# Optimizing a Trainium2 kernel written in Bass

```python
import numpy as np
import jax
import jax.numpy as jnp

def _softmax(x, axis=-1):
    return jax.nn.softmax(x, axis=axis)

def _gelu(x):
    return jax.nn.gelu(x, approximate=True)

def _silu(x):
    return jax.nn.silu(x)

def _sigmoid(x):
    return jax.nn.sigmoid(x)

def _layernorm(x, axis=-1, eps=1e-05):
    m = jnp.mean(x, axis=axis, keepdims=True)
    v = jnp.var(x, axis=axis, keepdims=True)
    return (x - m) / jnp.sqrt(v + eps)

def _scatter_add(tgt, idx, src, axis=0):
    return tgt.at[idx].add(src)

def _segment_sum(src, seg, n):
    return jax.ops.segment_sum(src, seg, n)
kernel_name = 'mk_prb_d1_jaxref_r8_8cc22e'

def setup_inputs(seed: int=0):
    np.random.seed(seed)
    _w = jnp.asarray

    def _L0_attn_setup():
        import jax, jax.numpy as jnp
        import numpy as np
        HID = 128
        NH = 4
        DK = 32
        DV = 64
        C = 64
        EPS = 1e-05
        GLN = 16.0

        def _xavier(key, shape, gain=2 ** (-2.5)):
            fan_in, fan_out = shape
            lim = gain * np.sqrt(6.0 / (fan_in + fan_out))
            return jax.random.uniform(key, shape, jnp.float32, -lim, lim)

        def _chunk_simple_gla(q, k, v, g):
            B, H, N, dk = q.shape
            dv = v.shape[-1]
            nc = N // C
            scale = dk ** (-0.5)
            q = q.reshape(B, H, nc, C, dk) * scale
            k = k.reshape(B, H, nc, C, dk)
            v = v.reshape(B, H, nc, C, dv)
            g = g.reshape(B, H, nc, C)
            gc = jnp.cumsum(g, axis=-1)
            gt = gc[..., -1]
            dec = gc[..., :, None] - gc[..., None, :]
            mask = jnp.tril(jnp.ones((C, C), bool))
            A = jnp.einsum('bhntd,bhnsd->bhnts', q, k)
            A = A * jnp.where(mask, jnp.exp(jnp.where(mask, dec, 0.0)), 0.0)
            o_intra = jnp.einsum('bhnts,bhnsd->bhntd', A, v)
            qs = jnp.moveaxis(q, 2, 0)
            ks_ = jnp.moveaxis(k, 2, 0)
            vs = jnp.moveaxis(v, 2, 0)
            gcs = jnp.moveaxis(gc, 2, 0)
            gts = jnp.moveaxis(gt, 2, 0)
            S0 = jnp.zeros((B, H, dk, dv), q.dtype)

            def step(S, inp):
                qc, kc, vc, gcc, gtc = inp
                o_int = jnp.einsum('bhtd,bhde->bhte', qc * jnp.exp(gcc)[..., None], S)
                kd = kc * jnp.exp(gtc[..., None] - gcc)[..., None]
                S = jnp.exp(gtc)[..., None, None] * S + jnp.einsum('bhtd,bhte->bhde', kd, vc)
                return (S, o_int)
            _, o_inter = jax.lax.scan(step, S0, (qs, ks_, vs, gcs, gts))
            o = o_intra + jnp.moveaxis(o_inter, 0, 2)
            return o.reshape(B, H, N, dv)
        key = jax.random.key(seed)
        ks = jax.random.split(key, 8)
        x = jax.random.normal(ks[0], (4, 256, HID), jnp.float32)
        Wq = _xavier(ks[1], (HID, NH * DK))
        Wk = _xavier(ks[2], (HID, NH * DK))
        Wv = _xavier(ks[3], (HID, NH * DV))
        Wg = _xavier(ks[4], (HID, NH * DV))
        Wgk = _xavier(ks[5], (HID, NH))
        bgk = jnp.zeros((NH,), jnp.float32)
        Wo = _xavier(ks[6], (NH * DV, HID))
        gnorm_w = jnp.ones((DV,), jnp.float32)
        return {'x': x, 'Wq': Wq, 'Wk': Wk, 'Wv': Wv, 'Wg': Wg, 'Wgk': Wgk, 'bgk': bgk, 'Wo': Wo, 'gnorm_w': gnorm_w}
    _L0_attn_in = _L0_attn_setup()

    def _L0_ffn_setup():
        import jax, jax.numpy as jnp
        import numpy as np
        NUM_EXPERTS = 8
        N_EMBD = 128
        D_FF = 4 * N_EMBD
        B, S = (4, 256)
        key = jax.random.key(seed)
        ks = jax.random.split(key, 6)
        x = jax.random.normal(ks[0], (B, S, N_EMBD), dtype=jnp.float32)
        gate_w = jax.random.normal(ks[1], (N_EMBD, NUM_EXPERTS), dtype=jnp.float32) * 0.02
        w1 = jax.random.normal(ks[2], (NUM_EXPERTS, N_EMBD, D_FF), dtype=jnp.float32) * 0.02
        b1 = jnp.zeros((NUM_EXPERTS, D_FF), dtype=jnp.float32)
        w2 = jax.random.normal(ks[3], (NUM_EXPERTS, D_FF, N_EMBD), dtype=jnp.float32) * 0.02
        b2 = jnp.zeros((NUM_EXPERTS, N_EMBD), dtype=jnp.float32)
        return {'x': x, 'gate_w': gate_w, 'w1': w1, 'b1': b1, 'w2': w2, 'b2': b2}
    _L0_ffn_in = _L0_ffn_setup()
    _d = {'L0_attn_x': _L0_attn_in['x'], 'L0_attn_Wq': _L0_attn_in['Wq'], 'L0_attn_Wk': _L0_attn_in['Wk'], 'L0_attn_Wv': _L0_attn_in['Wv'], 'L0_attn_Wg': _L0_attn_in['Wg'], 'L0_attn_Wgk': _L0_attn_in['Wgk'], 'L0_attn_bgk': _L0_attn_in['bgk'], 'L0_attn_Wo': _L0_attn_in['Wo'], 'L0_attn_gnorm_w': _L0_attn_in['gnorm_w'], 'L0_ffn_gate_w': _L0_ffn_in['gate_w'], 'L0_ffn_w1': _L0_ffn_in['w1'], 'L0_ffn_b1': _L0_ffn_in['b1'], 'L0_ffn_w2': _L0_ffn_in['w2'], 'L0_ffn_b2': _L0_ffn_in['b2']}
    _x0 = _d['L0_attn_x']
    _d['L0_attn_x'] = jax.random.normal(jax.random.fold_in(jax.random.key(seed), 1), (32, 256, 128), dtype=_x0.dtype)
    del _x0
    return _d

def reference(L0_attn_x, L0_attn_Wq, L0_attn_Wk, L0_attn_Wv, L0_attn_Wg, L0_attn_Wgk, L0_attn_bgk, L0_attn_Wo, L0_attn_gnorm_w, L0_ffn_gate_w, L0_ffn_w1, L0_ffn_b1, L0_ffn_w2, L0_ffn_b2):

    def _L0_attn_ref(x, Wq, Wk, Wv, Wg, Wgk, bgk, Wo, gnorm_w):
        import jax, jax.numpy as jnp
        import numpy as np
        HID = 128
        NH = 4
        DK = 32
        DV = 64
        C = 64
        EPS = 1e-05
        GLN = 16.0

        def _xavier(key, shape, gain=2 ** (-2.5)):
            fan_in, fan_out = shape
            lim = gain * np.sqrt(6.0 / (fan_in + fan_out))
            return jax.random.uniform(key, shape, jnp.float32, -lim, lim)

        def _chunk_simple_gla(q, k, v, g):
            B, H, N, dk = q.shape
            dv = v.shape[-1]
            nc = N // C
            scale = dk ** (-0.5)
            q = q.reshape(B, H, nc, C, dk) * scale
            k = k.reshape(B, H, nc, C, dk)
            v = v.reshape(B, H, nc, C, dv)
            g = g.reshape(B, H, nc, C)
            gc = jnp.cumsum(g, axis=-1)
            gt = gc[..., -1]
            dec = gc[..., :, None] - gc[..., None, :]
            mask = jnp.tril(jnp.ones((C, C), bool))
            A = jnp.einsum('bhntd,bhnsd->bhnts', q, k)
            A = A * jnp.where(mask, jnp.exp(jnp.where(mask, dec, 0.0)), 0.0)
            o_intra = jnp.einsum('bhnts,bhnsd->bhntd', A, v)
            qs = jnp.moveaxis(q, 2, 0)
            ks_ = jnp.moveaxis(k, 2, 0)
            vs = jnp.moveaxis(v, 2, 0)
            gcs = jnp.moveaxis(gc, 2, 0)
            gts = jnp.moveaxis(gt, 2, 0)
            S0 = jnp.zeros((B, H, dk, dv), q.dtype)

            def step(S, inp):
                qc, kc, vc, gcc, gtc = inp
                o_int = jnp.einsum('bhtd,bhde->bhte', qc * jnp.exp(gcc)[..., None], S)
                kd = kc * jnp.exp(gtc[..., None] - gcc)[..., None]
                S = jnp.exp(gtc)[..., None, None] * S + jnp.einsum('bhtd,bhte->bhde', kd, vc)
                return (S, o_int)
            _, o_inter = jax.lax.scan(step, S0, (qs, ks_, vs, gcs, gts))
            o = o_intra + jnp.moveaxis(o_inter, 0, 2)
            return o.reshape(B, H, N, dv)
        B, N, _ = x.shape
        q = (x @ Wq).reshape(B, N, NH, DK).transpose(0, 2, 1, 3)
        k = (x @ Wk).reshape(B, N, NH, DK).transpose(0, 2, 1, 3)
        v = (x @ Wv).reshape(B, N, NH, DV).transpose(0, 2, 1, 3)
        gk = (x @ Wgk + bgk).transpose(0, 2, 1)
        gk = jax.nn.log_sigmoid(gk) / GLN
        o = _chunk_simple_gla(q, k, v, gk)
        o = o.transpose(0, 2, 1, 3)
        g = (x @ Wg).reshape(B, N, NH, DV)
        on = o * jax.lax.rsqrt(jnp.mean(o * o, axis=-1, keepdims=True) + EPS) * gnorm_w
        o = on * (g * jax.nn.sigmoid(g))
        o = o.reshape(B, N, NH * DV)
        return o @ Wo

    def _L0_ffn_ref(x, gate_w, w1, b1, w2, b2):
        import jax, jax.numpy as jnp
        import numpy as np
        NUM_EXPERTS = 8
        N_EMBD = 128
        D_FF = 4 * N_EMBD
        B, S = (4, 256)
        Bb, Ss, D = x.shape
        x_flat = x.reshape(-1, D)
        router_logits = x_flat @ gate_w
        router_probs = jax.nn.softmax(router_logits, axis=-1)
        expert_idx = jnp.argmax(router_probs, axis=-1)
        expert_w = jnp.take_along_axis(router_probs, expert_idx[:, None], axis=1)[:, 0]
        out = jnp.zeros_like(x_flat)
        for e in range(NUM_EXPERTS):
            h = jax.nn.gelu(x_flat @ w1[e] + b1[e], approximate=False)
            y = h @ w2[e] + b2[e]
            sel = expert_idx == e
            out = out + jnp.where(sel, expert_w, 0.0)[:, None] * y
        return out.reshape(Bb, Ss, D)
    x = L0_attn_x
    xn = _layernorm(x, axis=-1)
    x = x + _L0_attn_ref(xn, L0_attn_Wq, L0_attn_Wk, L0_attn_Wv, L0_attn_Wg, L0_attn_Wgk, L0_attn_bgk, L0_attn_Wo, L0_attn_gnorm_w) + _L0_ffn_ref(xn, L0_ffn_gate_w, L0_ffn_w1, L0_ffn_b1, L0_ffn_w2, L0_ffn_b2)
    return x

_drawn_inputs = setup_inputs


def setup_inputs(seed=0):
    import zlib

    import numpy as np

    out = dict(_drawn_inputs(seed))
    spreads = {'L0_attn_bgk': (0.0, 0.8),
     'L0_attn_gnorm_w': (1.0, 0.6),
     'L0_ffn_b1': (0.0, 0.8),
     'L0_ffn_b2': (0.0, 0.47)}
    factors = {'L0_attn_Wq': 3.71,
     'L0_attn_Wk': 3.694,
     'L0_attn_Wv': 3.703,
     'L0_attn_Wg': 3.739,
     'L0_attn_Wgk': 8.0,
     'L0_attn_Wo': 3.706,
     'L0_ffn_gate_w': 3.027,
     'L0_ffn_w1': 6.117,
     'L0_ffn_w2': 5.565}
    for name, (base, spread) in spreads.items():
        noise = np.random.default_rng([zlib.crc32(name.encode()), seed]).standard_normal(out[name].shape)
        drawn = base * np.exp(spread * noise) if base else spread * noise
        out[name] = jnp.asarray(drawn.astype(out[name].dtype))
    for name, factor in factors.items():
        out[name] = (out[name] * factor).astype(out[name].dtype)
    return out
```

```python
from contextlib import ExitStack

import concourse.bass as bass
from concourse import mybir

ALU = mybir.AluOpType
ACT = mybir.ActivationFunctionType
AX = mybir.AxisListType
F32 = mybir.dt.float32
BF16 = mybir.dt.bfloat16
I32 = mybir.dt.int32

P = 128
LN_EPS = 1e-5
RMS_EPS = 1e-5
GATE_NORM = 16.0
MASKED = -1e30


def turn(i, j, d, n):
    return i + (j + d) // n, (j + d) % n


class Chain:

    def __init__(self, eng, sem, per_step):
        self.eng, self.sem, self.per_step = eng, sem, per_step

    def begin(self, step):
        self.base, self.n = step * self.per_step, 0

    def up(self, ins):
        ins.then_inc(self.sem, 1)
        self.n += 1

    def wait(self):
        self.eng.wait_ge(self.sem, self.base + self.n)

    def end(self):
        assert self.n == self.per_step


def build_layer(nc, x, Wq, Wk, Wv, Wg, Wgk, bgk, Wo, gnorm_w, gate_w, w1, b1, w2, b2, out):
    SEQS, SEQ, D = x.shape
    TOKENS = SEQS * SEQ
    TILES = TOKENS // P
    H = Wgk.shape[1]
    DK = Wq.shape[1] // H
    DV = Wv.shape[1] // H
    HV = H * DV
    EXP, _, FF = w1.shape
    FC = FF // P
    NL = EXP + H
    assert D == P and H * DK == P and SEQ == 2 * P and HV == 2 * P and FF == 4 * P

    GT = 4
    GROUPS = TILES // GT
    BLOCKS = -(-(TILES + EXP - 1) // 4) * 4
    XW = D + 1
    WB = FF + FC
    PAD = TILES // 2 * EXP
    TE = TILES * EXP
    TH = TILES * H

    x_t = x.rearrange("s (k p) d -> p (s k) d", p=P)
    x_rows = x_t
    out_rows = out.rearrange("s n d -> (s n) d")
    out_t = out.rearrange("s (k p) d -> p (s k) d", p=P)
    xw_dram = nc.dram_tensor("xn_and_weight", [TOKENS, XW], F32).ap()
    xw_t = xw_dram.rearrange("(t p) c -> p t c", p=P)
    xt_dram = nc.dram_tensor("xn_transposed", [GROUPS, P, GT * P], F32).ap()
    gc_dram = nc.dram_tensor("decay_rows", [TH, P], F32).ap()

    with ExitStack() as ctx:
        def sb(name, shape, dt=F32):
            return ctx.enter_context(nc.sbuf_tensor(name, shape, dt))

        def ps(name, shape):
            return ctx.enter_context(nc.psum_tensor(name, shape, F32))

        def sem(name):
            return ctx.enter_context(nc.semaphore(name))

        ident = sb("ident", [P, P])
        upto = sb("upto", [P, P])
        onesf = sb("onesf", [P, P])
        before = sb("before", [P, P], BF16)
        onesb = sb("onesb", [P, P], BF16)
        iota_i = sb("iota_i", [P, P], I32)
        iota_f = sb("iota_f", [P, P])
        part_i = sb("part_i", [P, 1], I32)
        part1 = sb("part1", [P, 1])
        rev_i = sb("rev_i", [P, EXP], I32)
        rev = sb("rev", [P, EXP])
        neg_half = sb("neg_half", [P, 8])
        headmask = sb("headmask", [P, HV])
        wq_sb = sb("wq_sb", [P, H * DK])
        wk_sb = sb("wk_sb", [P, H * DK])
        wvg_sb = sb("wvg_sb", [P, 2 * HV])
        wr_sb = sb("wr_sb", [P, NL])
        wo_raw = sb("wo_raw", [P, 2, D])
        wo_sb = sb("wo_sb", [P, 2, D])
        gn_col = sb("gn_col", [P, 1])
        bgk_bc = sb("bgk_bc", [P, H])
        b2_bc = sb("b2_bc", [P, EXP, D])
        b1_rows = sb("b1_rows", [EXP * FC, P])
        w1b = sb("w1b", [P, EXP, WB])
        w2_sb = sb("w2_sb", [P, EXP, FC, D])

        x_all = sb("x_all", [P, TILES, D])
        stats = [sb(f"stats{q}", [P, GT, 6]) for q in range(4)]
        mv = [sb(f"mv{q}", [P, GT, 2]) for q in range(4)]
        vpe = [sb(f"vpe{q}", [P, GT]) for q in range(4)]
        rstd = [sb(f"rstd{q}", [P, GT]) for q in range(4)]
        nmr = [sb(f"nmr{q}", [P, GT]) for q in range(4)]
        xw = [sb(f"xw{q}", [P, GT, XW]) for q in range(4)]
        xts = [sb(f"xts{q}", [P, GT * P]) for q in range(2)]
        lg_all = sb("lg_all", [P, TILES, NL])
        lmax = [sb(f"lmax{q}", [P, GT]) for q in range(4)]
        d_all = sb("d_all", [P, TILES, EXP])
        ex = [sb(f"ex{q}", [P, GT, EXP]) for q in range(4)]
        sumex = [sb(f"sumex{q}", [P, GT]) for q in range(4)]

        z = sb("z", [P, TILES, H])
        az = sb("az", [P, TH])
        ez = sb("ez", [P, TH])
        l1 = sb("l1", [P, TH])
        g_all = sb("g_all", [P, TH])
        gc = sb("gc", [P, TILES, H])
        gdiff = sb("gdiff", [P, TH])
        e_k = sb("e_k", [P, TILES, H])
        e_q = sb("e_q", [P, TILES, H])
        gcT = sb("gcT", [P, 2, P])
        val = sb("val", [P, TILES, EXP])
        vmax = sb("vmax", [P, TILES])
        onehot = sb("onehot", [P, TILES, EXP], BF16)
        pre = [sb(f"pre{q}", [P, PAD + TE]) for q in range(2)]
        tot_i = sb("tot_i", [P, EXP], I32)
        nb_i = sb("nb_i", [P, EXP], I32)
        cb = [sb(f"cb{q}", [P, 2 * EXP]) for q in range(2)]
        base = sb("base", [P, EXP])
        slot_f = sb("slot_f", [P, TILES, EXP])
        pos = sb("pos", [P, TILES])
        pos_i = sb("pos_i", [P, TILES], I32)
        lo_i = sb("lo_i", [P, TILES], I32)
        hi_i = sb("hi_i", [P, TILES], I32)
        lo = sb("lo", [P, TILES])
        hi = sb("hi", [P, TILES])
        row1h = w2_sb[:].rearrange("p e c d -> p (e c d)").bitcast(BF16).rearrange("p (t r) -> p t r", r=P)
        blk1h = w1b[:].rearrange("p e n -> p (e n)").bitcast(BF16)[:, 0:TILES * BLOCKS].rearrange("p (t b) -> p t b", b=BLOCKS)
        blkval = sb("blkval", [P, TILES, 2, BLOCKS], BF16)
        part1_of = sb("part1_of", [P, BLOCKS])
        id1 = sb("id1", [P, BLOCKS])
        empty = sb("empty", [P, BLOCKS])
        gid = sb("gid", [P, BLOCKS], I32)
        sid = sb("sid", [P, BLOCKS], I32)
        isge = sb("isge", [P, BLOCKS, EXP - 1])
        be_f = sb("be_f", [P, BLOCKS])
        be = sb("be", [P, BLOCKS], I32)

        xT = [sb(f"xT{j}", [P, SEQ]) for j in range(2)]
        gcB = [sb(f"gcB{j}", [P, 2 * H, P]) for j in range(2)]
        E = [sb(f"E{j}", [P, 2, H * P]) for j in range(2)]
        qb = sb("qb", [P, 2, H, P])
        qT1 = [sb(f"qT1{j}", [P, P]) for j in range(2)]
        kT = sb("kT", [P, SEQ])
        v_sb = [sb(f"v_sb{j}", [P, 2, HV]) for j in range(2)]
        th = sb("th", [P, 2, HV])
        gate = [sb(f"gate{j}", [P, 2, HV]) for j in range(2)]
        kd = sb("kd", [P, H * DK])
        S_sb = sb("S_sb", [P, HV])
        pr = sb("pr", [P, 2, H * P])
        inter = sb("inter", [P, HV])
        oo = sb("oo", [P, 2, HV])
        sq = sb("sq", [P, 2, HV])
        ms = sb("ms", [P, 2 * H])
        msn = sb("msn", [P, 2 * H])
        rms = sb("rms", [P, 2 * H])
        og = sb("og", [P, 2, HV])
        on = sb("on", [P, 2, HV])
        oT = sb("oT", [P, 4, P])
        res = [sb(f"res{j}", [P, 2, D]) for j in range(2)]

        gidx = [sb(f"gidx{j}", [P, 1], I32) for j in range(4)]
        sidx = [sb(f"sidx{j}", [P, 1], I32) for j in range(4)]
        xg = [sb(f"xg{j}", [P, XW]) for j in range(4)]
        xgT = [sb(f"xgT{j}", [P, P]) for j in range(2)]
        wbuf = [E[j][:].rearrange("p k n -> p (k n)")[:, 0:WB] for j in range(2)]
        hid = [gcB[j][:, 0:FC, :] for j in range(2)]
        yb = [sb(f"yb{j}", [P, D]) for j in range(2)]
        yw = [sb(f"yw{j}", [P, D]) for j in range(4)]

        psQK = ps("psQK", [P, 512])
        psVG = ps("psVG", [P, 2, 512])
        psKS = ps("psKS", [P, 512])
        psA = ps("psA", [P, 2, 512])
        psO = ps("psO", [P, 512])
        psT = ps("psT", [P, 512])

        x_loaded = [sem(f"x_loaded{q}") for q in range(4)]
        small_loaded = sem("small_loaded")
        proj_loaded = sem("proj_loaded")
        expert_loaded = sem("expert_loaded")
        w_loaded = sem("w_loaded")
        xw_stored = [sem(f"xw_stored{q}") for q in range(4)]
        xt_stored = [sem(f"xt_stored{q}") for q in range(2)]
        gc_stored = sem("gc_stored")
        xT_loaded = [sem(f"xT_loaded{j}") for j in range(2)]
        gcB_loaded = [sem(f"gcB_loaded{j}") for j in range(2)]
        res_stored = [sem(f"res_stored{j}") for j in range(2)]
        gathered = [sem(f"gathered{j}") for j in range(4)]
        scattered = [sem(f"scattered{j}") for j in range(4)]
        pool_consts = sem("pool_consts")
        consts = sem("consts")
        dve_stats = sem("dve_stats")
        rstd_ready = sem("rstd_ready")
        nmr_ready = sem("nmr_ready")
        xn_ready = sem("xn_ready")
        xt_ps_ready = sem("xt_ps_ready")
        xts_ready = sem("xts_ready")
        lg_ready = sem("lg_ready")
        dve_max = sem("dve_max")
        ex_ready = sem("ex_ready")
        dve_weight = sem("dve_weight")
        dve_route = sem("dve_route")
        act_route = sem("act_route")
        pe_route = sem("pe_route")
        qk_ready = sem("qk_ready")
        vg_ready = sem("vg_ready")
        a_ready = sem("a_ready")
        k0_ready = sem("k0_ready")
        s_ready = sem("s_ready")
        o_ready = sem("o_ready")
        inter_ready = sem("inter_ready")
        oT_ps_ready = sem("oT_ps_ready")
        wo_ready = sem("wo_ready")
        qk_copied = sem("qk_copied")
        v_copied = sem("v_copied")
        o_copied = sem("o_copied")
        e_ready = sem("e_ready")
        oT_copied = sem("oT_copied")
        dve_comb = sem("dve_comb")
        p_ready = sem("p_ready")
        kd_ready = sem("kd_ready")
        dve_on = sem("dve_on")
        s_copied = sem("s_copied")
        gate_ready = sem("gate_ready")
        res_ready = sem("res_ready")
        pool_dec = sem("pool_dec")
        rms_ready = sem("rms_ready")
        tick = sem("tick")
        gidx_ready = sem("gidx_ready")
        sidx_ready = sem("sidx_ready")
        xgT_ps_ready = sem("xgT_ps_ready")
        xgT_copied = sem("xgT_copied")
        w_copied = sem("w_copied")
        h_ready = sem("h_ready")
        gelu_done = sem("gelu_done")
        y_ready = sem("y_ready")
        dve_y = sem("dve_y")

        STATS_N, MAX_N, WEIGHT_N = 9, 3, 2
        COMB_N, ON_N, Y_N = 5, 2, 2
        LAST = SEQS - 1
        FIRST_SEQS = 2

        block = ctx.enter_context(nc.Block())

        @block.sync
        def _(sp):
            def load_x(i, q):
                if not (isinstance(i, int) and i == 0):
                    sp.wait_ge(x_loaded[q], i * 16)
                g = i * 4 + q
                sp.dma_start(x_all[:, bass.ds(g * GT, GT), :], x_t[:, bass.ds(g * GT, GT), :]).then_inc(x_loaded[q], 16)

            def store_xt(i, q):
                g = i * 4 + q
                sp.wait_ge(xts_ready, g + 1)
                sp.dma_start(xt_dram[bass.ds(g, 1), :, :].rearrange("a p n -> p (a n)"), xts[q % 2][:]).then_inc(xt_stored[q % 2], 16)

            def store_xw(i, q):
                g = i * 4 + q
                sp.wait_ge(dve_weight, (g + 1) * WEIGHT_N)
                sp.dma_start(xw_t[:, bass.ds(g * GT, GT), :], xw[q][:]).then_inc(xw_stored[q], 16)

            def norm_step(i, q):
                if not (isinstance(i, int) and i + 1 >= GROUPS // 4):
                    load_x(i + 1, q)
                if not (isinstance(i, int) and i * 4 + q < 1):
                    store_xt(*turn(i, q, -1, 4))
                if not (isinstance(i, int) and i * 4 + q < 3):
                    store_xw(*turn(i, q, -3, 4))

            for q in range(4):
                load_x(0, q)
            for q in range(4):
                norm_step(0, q)
            with sp.Fori(1, GROUPS // 4 - 1) as i:
                for q in range(4):
                    norm_step(i, q)
            for q in range(4):
                norm_step(GROUPS // 4 - 1, q)
            store_xt(GROUPS // 4 - 1, 3)
            for q in range(1, 4):
                store_xw(GROUPS // 4 - 1, q)

            sp.dma_start(b1_rows[:], b1.rearrange("e (c f) -> (e c) f", f=P)).then_inc(expert_loaded, 16)
            sp.dma_start(b2_bc[:].rearrange("p e d -> p (e d)"),
                         b2.rearrange("e d -> (e d)").partition_broadcast(P)).then_inc(expert_loaded, 16)
            sp.wait_ge(dve_route, ROUTE["gcT"])
            sp.dma_start(gc_dram.rearrange("(a p) t -> p a t", p=P), gcT[:]).then_inc(gc_stored, 16)
            sp.wait_ge(pe_route, 4)
            sp.dma_start(w1b[:, :, 0:FF], w1.rearrange("e d f -> d e f")).then_inc(w_loaded, 16)
            for e in range(EXP):
                sp.dma_start(w2_sb[:, e, :, :], w2[e].rearrange("(c f) d -> f c d", f=P)).then_inc(w_loaded, 16)


            def load_seq(i, j):
                s = i * 2 + j
                sp.dma_start(xT[j][:], xt_dram[bass.ds(i, 1), :, j * SEQ:(j + 1) * SEQ].rearrange("a p n -> p (a n)")).then_inc(xT_loaded[j], 16)
                sp.dma_start(gcB[j][:].rearrange("p h t -> p (h t)"),
                             gc_dram[bass.ds(s * 2 * H, 2 * H), :].rearrange("r t -> (r t)").partition_broadcast(P)).then_inc(gcB_loaded[j], 16)

            def store_res(i, j):
                s = i * 2 + j
                sp.wait_ge(res_ready, s + 1)
                sp.dma_start(out_t[:, bass.ds(s * 2, 2), :], res[j][:]).then_inc(res_stored[j], 16)

            for q in range(4):
                sp.wait_ge(xw_stored[q], GROUPS // 4 * 16)
            for q in range(2):
                sp.wait_ge(xt_stored[q], GROUPS // 2 * 16)
            sp.wait_ge(gc_stored, 16)
            for j in range(2):
                load_seq(0, j)

            def step(i, j):
                s = i * 2 + j
                sp.wait_ge(k0_ready, s + 1)
                sp.wait_ge(e_ready, s + 1)
                load_seq(i + 1, j)

            for j in range(2):
                step(0, j)
            with sp.Fori(1, SEQS // 2 - 1) as i:
                for j in range(2):
                    store_res(i - 1, j)
                    step(i, j)
            for j in range(2):
                store_res(SEQS // 2 - 2, j)
            for j in range(2):
                store_res(SEQS // 2 - 1, j)
            for j in range(2):
                sp.wait_ge(res_stored[j], SEQS // 2 * 16)
            sp.wait_ge(w_loaded, (EXP + 1) * 16)

        @block.gpsimd
        def _(pool):
            c = [0]

            def const(ins):
                ins.then_inc(pool_consts, 1)
                c[0] += 1

            const(nc.gpsimd.memset(ident[:], 1.0))
            const(nc.gpsimd.memset(upto[:], 1.0))
            const(nc.gpsimd.memset(onesf[:], 1.0))
            const(nc.gpsimd.memset(before[:], 1.0))
            const(nc.gpsimd.memset(onesb[:], 1.0))
            const(nc.gpsimd.memset(neg_half[:], -0.5))
            const(nc.gpsimd.memset(headmask[:], 0.0))
            const(nc.gpsimd.memset(qb[:], 0.0))
            for q in range(2):
                const(nc.gpsimd.memset(pre[q][:, 0:PAD], 0.0))
                const(nc.gpsimd.memset(cb[q][:, 0:EXP], 0.0))
            const(nc.gpsimd.iota(iota_i[:], pattern=[[1, P]], base=0, channel_multiplier=0))
            const(nc.gpsimd.iota(part_i[:], pattern=[[0, 1]], base=1, channel_multiplier=1))
            const(nc.gpsimd.iota(rev_i[:], pattern=[[-1, EXP]], base=EXP, channel_multiplier=0))
            pool.wait_ge(pool_consts, c[0])
            const(nc.gpsimd.affine_select(out=ident[:], in_=ident[:], pattern=[[1, P]], compare_op=ALU.is_equal,
                                          fill=0.0, base=0, channel_multiplier=-1))
            const(nc.gpsimd.affine_select(out=upto[:], in_=upto[:], pattern=[[1, P]], compare_op=ALU.is_ge,
                                          fill=0.0, base=0, channel_multiplier=-1))
            const(nc.gpsimd.affine_select(out=before[:], in_=before[:], pattern=[[1, P]], compare_op=ALU.is_ge,
                                          fill=0.0, base=-1, channel_multiplier=-1))
            for h in range(H):
                pool.wait_ge(pool_consts, c[0])
                const(nc.gpsimd.memset(headmask[h * DK:(h + 1) * DK, h * DV:(h + 1) * DV], 1.0))
            assert c[0] == POOL_CONSTS

            def rstd_step(i, q):
                g = i * 4 + q
                pool.wait_ge(dve_stats, (g + 1) * STATS_N)
                nc.gpsimd.tensor_tensor(rstd[q][:], vpe[q][:], neg_half[:, 0:GT], ALU.pow).then_inc(rstd_ready, 1)

            pool.wait_ge(pool_consts, c[0])
            for q in range(4):
                rstd_step(0, q)
            with pool.Fori(1, GROUPS // 4) as i:
                for q in range(4):
                    pool.wait_ge(xn_ready, i * 4 + q - 3)
                    rstd_step(i, q)

            def dec(i, j):
                s = i * 2 + j
                pool.wait_ge(gcB_loaded[j], (i + 1) * 16)
                nc.gpsimd.tensor_tensor(gcB[j][:], gcB[j][:],
                                        gc[:, bass.ds(s * 2, 2), :].rearrange("p k h -> p (k h)").unsqueeze(2).to_broadcast([P, 2 * H, P]),
                                        ALU.subtract).then_inc(pool_dec, 1)
                pool.wait_ge(pool_dec, s * 2 + 1)
                pool.sem_inc(tick, 1)
                nc.gpsimd.affine_select(out=gcB[j][:], in_=gcB[j][:], pattern=[[0, 2 * H], [1, P]], compare_op=ALU.is_ge,
                                        fill=MASKED, base=0, channel_multiplier=-1).then_inc(pool_dec, 1)

            def rms_step(i, j):
                s = i * 2 + j
                pool.wait_ge(dve_comb, (s + 1) * COMB_N)
                nc.gpsimd.tensor_tensor(rms[:], msn[:], neg_half[:, 0:2 * H], ALU.pow).then_inc(rms_ready, 1)

            pool.wait_ge(dve_route, ROUTE["gc"])
            dec(0, 0)
            dec(0, 1)
            rms_step(0, 0)
            dec(1, 0)
            with pool.Fori(1, SEQS // 2 - 1) as i:
                for j in range(2):
                    pool.wait_ge(dve_on, (i * 2 + j - 1) * ON_N)
                    rms_step(*turn(i, j, -1, 2))
                    dec(*turn(i, j, 1, 2))
            last = SEQS // 2 - 1
            pool.wait_ge(dve_on, (LAST - 2) * ON_N)
            rms_step(last - 1, 1)
            dec(last, 1)
            pool.wait_ge(dve_on, (LAST - 1) * ON_N)
            rms_step(last, 0)
            pool.wait_ge(dve_on, LAST * ON_N)
            rms_step(last, 1)

            def gather(i, j):
                b = i * 4 + j
                pool.wait_ge(gidx_ready, b + 1)
                pool.sem_inc(tick, 1)
                nc.gpsimd.indirect_dma_start(out=xg[j][:], out_offset=None, in_=xw_dram,
                                             in_offset=bass.IndirectOffsetOnAxis(ap=gidx[j][:], axis=0)).then_inc(gathered[j], 16)

            def scatter(i, j):
                b = i * 4 + j
                pool.wait_ge(dve_y, (b + 1) * Y_N)
                pool.wait_ge(sidx_ready, b + 1)
                pool.sem_inc(tick, 1)
                nc.gpsimd.indirect_dma_start(out=out_rows, out_offset=bass.IndirectOffsetOnAxis(ap=sidx[j][:], axis=0),
                                             in_=yw[j][:], in_offset=None, bounds_check=TOKENS - 1, oob_is_err=False,
                                             compute_op=ALU.add).then_inc(scattered[j], 16)

            for q in range(4):
                pool.wait_ge(xw_stored[q], GROUPS // 4 * 16)
            for j in range(3):
                gather(0, j)
            for j in range(2):
                pool.wait_ge(res_stored[j], SEQS // 2 * 16)
            gather(0, 3)
            scatter(0, 0)
            for j in range(1, 4):
                pool.wait_ge(dve_y, j * Y_N)
                gather(*turn(0, j, 3, 4))
                scatter(0, j)
            with pool.Fori(1, BLOCKS // 4 - 1) as i:
                for j in range(4):
                    pool.wait_ge(dve_y, (i * 4 + j) * Y_N)
                    gather(*turn(i, j, 3, 4))
                    scatter(i, j)
            last = BLOCKS // 4 - 1
            pool.wait_ge(dve_y, last * 4 * Y_N)
            gather(last, 3)
            for j in range(4):
                scatter(last, j)
            for j in range(4):
                pool.wait_ge(scattered[j], BLOCKS // 4 * 16)

        @block.tensor
        def _(pe):
            def transposes(i, q):
                g = i * 4 + q
                pe.wait_ge(xn_ready, g + 1)
                if not (isinstance(i, int) and g < 2):
                    pe.wait_ge(xts_ready, g - 1)
                for k in range(GT):
                    last = nc.tensor.transpose(psA[:, q % 2, k * P:(k + 1) * P], xw[q][:, k, 0:D], ident[:])
                last.then_inc(xt_ps_ready, 1)

            def logits(i, q):
                g = i * 4 + q
                pe.wait_ge(xts_ready, g + 1)
                if not (isinstance(i, int) and g < 2):
                    pe.wait_ge(dve_max, (g - 1) * MAX_N)
                for k in range(GT):
                    last = nc.tensor.matmul(psVG[:, q % 2, k * NL:(k + 1) * NL], xts[q % 2][:, k * P:(k + 1) * P], wr_sb[:],
                                            start=True, stop=True)
                last.then_inc(lg_ready, 1)

            pe.wait_ge(pool_consts, POOL_CONSTS)
            pe.wait_ge(small_loaded, SMALL * 16)
            transposes(0, 0)
            for q in range(1, 4):
                transposes(0, q)
                logits(0, q - 1)
            with pe.Fori(1, GROUPS // 4) as i:
                for q in range(4):
                    transposes(i, q)
                    logits(*turn(i, q, -1, 4))
            logits(GROUPS // 4 - 1, 3)

            pe.wait_ge(dve_route, ROUTE["g"])
            nc.tensor.matmul(psQK[:, 0:TH], upto[:], g_all[:], start=True, stop=True)
            nc.tensor.matmul(psQK[:, TH:2 * TH], onesf[:], g_all[:], start=True, stop=True).then_inc(pe_route, 1)
            pe.wait_ge(dve_route, ROUTE["onehot"])
            oh = onehot[:].rearrange("p t e -> p (t e)")
            nc.tensor.matmul(psKS[:, 0:TE], before[:], oh, start=True, stop=True)
            nc.tensor.matmul(psT[:, 0:TE], onesb[:], oh, start=True, stop=True).then_inc(pe_route, 1)
            pe.wait_ge(dve_route, ROUTE["gc"])
            gc_flat = gc[:].rearrange("p t h -> p (t h)")
            for a in range(2):
                nc.tensor.transpose(psO[:, a * P:(a + 1) * P], gc_flat[:, a * P:(a + 1) * P], ident[:])
            pe.wait_ge(expert_loaded, 2 * 16)
            nc.tensor.transpose(psO[:, 2 * P:2 * P + EXP * FC], b1_rows[:], ident[0:EXP * FC, 0:EXP * FC]).then_inc(pe_route, 1)
            pe.wait_ge(dve_route, ROUTE["blkval"])

            def place(t, start, stop):
                return nc.tensor.matmul(psA[:, 1, 0:2 * BLOCKS], row1h[:, bass.ds(t, 1), :].rearrange("p a r -> p (a r)"),
                                        blkval[:, bass.ds(t, 1), :, :].rearrange("p a v b -> p (a v b)"), start=start, stop=stop)

            place(0, True, False)
            with pe.Fori(0, (TILES - 4) // 4) as i:
                for k in range(4):
                    place(i * 4 + (k + 1), False, False)
            for t in range(TILES - 3, TILES - 1):
                place(t, False, False)
            place(TILES - 1, False, True).then_inc(pe_route, 1)

            def proj(i, j):
                s = i * 2 + j
                pe.wait_ge(xT_loaded[j], (i + 1) * 16)
                first = isinstance(i, int) and s == 0
                if not first:
                    pe.wait_ge(qk_copied, s)
                nc.tensor.matmul(psQK[:, 0:SEQ], wq_sb[:], xT[j][:], start=True, stop=True)
                nc.tensor.matmul(psQK[:, SEQ:2 * SEQ], wk_sb[:], xT[j][:], start=True, stop=True).then_inc(qk_ready, 1)
                if not first:
                    pe.wait_ge(v_copied, s)
                    pe.wait_ge(gate_ready, s)
                for k in range(2):
                    last = nc.tensor.matmul(psVG[:, k, :], xT[j][:, k * P:(k + 1) * P], wvg_sb[:], start=True, stop=True)
                last.then_inc(vg_ready, 1)

            def scores(i, j):
                s = i * 2 + j
                pe.wait_ge(qk_copied, s + 1)
                if not (isinstance(i, int) and s == 0):
                    pe.wait_ge(p_ready, s * 2)
                for k in range(2):
                    nc.tensor.matmul(psA[:, k, :], kT[:, k * P:(k + 1) * P], qb[:, k, :, :].rearrange("p h t -> p (h t)"),
                                     start=True, stop=True).then_inc(a_ready, 1)
                if not (isinstance(i, int) and s == 0):
                    pe.wait_ge(dve_comb, (s - 1) * COMB_N + 1)
                nc.tensor.matmul(psKS[:, 0:P], xT[j][:, 0:P], wk_sb[:], start=True, stop=True).then_inc(k0_ready, 1)

            def outputs(i, j):
                s = i * 2 + j
                pe.wait_ge(kd_ready, s + 1)
                pe.wait_ge(v_copied, s + 1)
                nc.tensor.matmul(psKS[:, HV:2 * HV], kd[:], v_sb[j][:, 0, :], start=True, stop=True).then_inc(s_ready, 1)
                if not (isinstance(i, int) and s == 0):
                    pe.wait_ge(o_copied, s)
                for k in range(2):
                    pe.wait_ge(p_ready, s * 2 + k + 1)
                    for h in range(H):
                        last = nc.tensor.matmul(psO[:, k * HV + h * DV:k * HV + (h + 1) * DV], pr[:, k, h * P:(h + 1) * P],
                                                v_sb[j][:, k, h * DV:(h + 1) * DV], start=True, stop=True)
                last.then_inc(o_ready, 1)
                pe.wait_ge(s_copied, s + 1)
                nc.tensor.matmul(psKS[:, 0:HV], qT1[j][:], S_sb[:], start=True, stop=True).then_inc(inter_ready, 1)

            def transpose_on(i, j):
                s = i * 2 + j
                pe.wait_ge(dve_on, (s + 1) * ON_N)
                if not (isinstance(i, int) and s == 0):
                    pe.wait_ge(res_ready, s)
                for k in range(2):
                    for a in range(2):
                        last = nc.tensor.transpose(psT[:, (2 * k + a) * P:(2 * k + a + 1) * P], on[:, k, a * P:(a + 1) * P], ident[:])
                last.then_inc(oT_ps_ready, 1)

            def project_out(i, j):
                s = i * 2 + j
                pe.wait_ge(oT_copied, s + 1)
                for k in range(2):
                    for a in range(2):
                        last = nc.tensor.matmul(psT[:, k * D:(k + 1) * D], oT[:, 2 * k + a, :], wo_sb[:, a, :],
                                                start=(a == 0), stop=(a == 1))
                last.then_inc(wo_ready, 1)

            def step(i, j):
                scores(i, j)
                project_out(*turn(i, j, -2, 2))
                proj(*turn(i, j, 1, 2))
                outputs(i, j)
                transpose_on(*turn(i, j, -1, 2))

            pe.wait_ge(dve_route, ROUTE["all"])
            pe.wait_ge(proj_loaded, 16 * 5)
            proj(0, 0)
            scores(0, 0)
            proj(0, 1)
            outputs(0, 0)
            scores(0, 1)
            proj(1, 0)
            outputs(0, 1)
            transpose_on(0, 0)
            with pe.Fori(1, SEQS // 2 - 1) as i:
                for j in range(2):
                    step(i, j)
            last = SEQS // 2 - 1
            step(last, 0)
            scores(last, 1)
            project_out(last - 1, 1)
            outputs(last, 1)
            transpose_on(last, 0)
            project_out(last, 0)
            transpose_on(last, 1)
            project_out(last, 1)

            psXT = [psQK, psKS]
            psY = [psO, psT]

            def transpose_rows(i, j):
                b = i * 4 + j
                pe.wait_ge(gathered[j], (i + 1) * 16)
                if not (isinstance(i, int) and b < 2):
                    pe.wait_ge(xgT_copied, b - 1)
                nc.tensor.transpose(psXT[j % 2][:, 0:P], xg[j][:, 0:D], ident[:]).then_inc(xgT_ps_ready, 1)

            def layer1(i, j):
                b = i * 4 + j
                pe.wait_ge(xgT_copied, b + 1)
                pe.wait_ge(w_copied, b + 1)
                if not (isinstance(i, int) and b < 2):
                    pe.wait_ge(gelu_done, b - 1)
                for c in range(FC):
                    last = nc.tensor.matmul(psVG[:, j % 2, c * P:(c + 1) * P], wbuf[j % 2][:, c * P:(c + 1) * P], xgT[j % 2][:],
                                            start=True, stop=True)
                last.then_inc(h_ready, 1)

            def layer2(i, j):
                b = i * 4 + j
                e = pe.value_load(be[0:1, bass.ds(b, 1)], min_val=0, max_val=EXP - 1)
                pe.wait_ge(gelu_done, b + 1)
                if not (isinstance(i, int) and b < 2):
                    pe.wait_ge(dve_y, (b - 2) * Y_N + 1)
                for c in range(FC):
                    last = nc.tensor.matmul(psY[j % 2][:, 0:D], hid[j % 2][:, c, :],
                                            w2_sb[:, bass.ds(e, 1), c, :].rearrange("p a d -> p (a d)"),
                                            start=(c == 0), stop=(c == FC - 1))
                last.then_inc(y_ready, 1)

            pe.wait_ge(res_ready, SEQS)
            pe.wait_ge(dve_comb, SEQS * COMB_N)
            pe.wait_ge(gate_ready, SEQS)
            pe.wait_ge(w_loaded, (EXP + 1) * 16)
            transpose_rows(0, 0)
            layer1(0, 0)
            transpose_rows(0, 1)
            for j in range(1, 4):
                layer1(0, j)
                transpose_rows(*turn(0, j, 1, 4))
                layer2(0, j - 1)
            with pe.Fori(1, BLOCKS // 4 - 1) as i:
                for j in range(4):
                    layer1(i, j)
                    transpose_rows(*turn(i, j, 1, 4))
                    layer2(*turn(i, j, -1, 4))
            last = BLOCKS // 4 - 1
            for j in range(4):
                layer1(last, j)
                if j < 3:
                    transpose_rows(last, j + 1)
                layer2(*turn(last, j, -1, 4))
            layer2(last, 3)

        @block.scalar
        def _(act):
            act.dma_start(wr_sb[:, 0:EXP], gate_w).then_inc(small_loaded, 16)
            act.dma_start(wr_sb[:, EXP:NL], Wgk).then_inc(small_loaded, 16)
            act.dma_start(bgk_bc[:], bgk.partition_broadcast(P)).then_inc(small_loaded, 16)
            for a in range(2):
                act.dma_start(gn_col[a * DV:(a + 1) * DV, :], gnorm_w.rearrange("(d a) -> d a", a=1)).then_inc(small_loaded, 16)
            act.dma_start(wo_raw[:], Wo.rearrange("(a p) d -> p a d", p=P)).then_inc(proj_loaded, 16)
            act.dma_start(wq_sb[:], Wq).then_inc(proj_loaded, 16)
            act.dma_start(wk_sb[:], Wk).then_inc(proj_loaded, 16)
            act.dma_start(wvg_sb[:, 0:HV], Wv).then_inc(proj_loaded, 16)
            act.dma_start(wvg_sb[:, HV:2 * HV], Wg).then_inc(proj_loaded, 16)

            def copy_xt(i, q):
                g = i * 4 + q
                act.wait_ge(xt_ps_ready, g + 1)
                if not (isinstance(i, int) and g < 2):
                    s2, t2 = (q % 2, i * 2 + q // 2)
                    act.wait_ge(xt_stored[s2], t2 * 16)
                    act.wait_ge(lg_ready, g - 1)
                nc.scalar.copy(xts[q % 2][:], psA[:, q % 2, :]).then_inc(xts_ready, 1)

            def exp_step(i, q):
                g = i * 4 + q
                act.wait_ge(dve_max, (g + 1) * MAX_N)
                nc.scalar.activation(ex[q][:], d_all[:, bass.ds(g * GT, GT), :], ACT.Exp).then_inc(ex_ready, 1)

            def apply_norm(i, q):
                g = i * 4 + q
                act.wait_ge(nmr_ready, g + 1)
                if not (isinstance(i, int) and i == 0):
                    act.wait_ge(xw_stored[q], i * 16)
                for k in range(GT):
                    last = nc.scalar.activation(xw[q][:, k, 0:D], x_all[:, bass.ds(g * GT + k, 1), :].rearrange("p a d -> p (a d)"),
                                                ACT.Identity, bias=nmr[q][:, k:k + 1], scale=rstd[q][:, k:k + 1])
                last.then_inc(xn_ready, 1)

            def norm_step(i, q):
                if not (isinstance(i, int) and i * 4 + q < 3):
                    exp_step(*turn(i, q, -3, 4))
                apply_norm(i, q)
                if not (isinstance(i, int) and i * 4 + q < 1):
                    copy_xt(*turn(i, q, -1, 4))

            for q in range(4):
                norm_step(0, q)
            with act.Fori(1, GROUPS // 4) as i:
                for q in range(4):
                    norm_step(i, q)
            last = GROUPS // 4 - 1
            exp_step(last, 1)
            copy_xt(last, 3)
            exp_step(last, 2)
            exp_step(last, 3)

            act.wait_ge(dve_route, ROUTE["az"])
            nc.scalar.activation(ez[:], az[:], ACT.Exp, scale=-1.0).then_inc(act_route, 1)
            act.wait_ge(act_route, 1)
            nc.scalar.activation(l1[:], ez[:], ACT.Ln, bias=onesf[:, 0:1]).then_inc(act_route, 1)
            act.wait_ge(dve_route, ROUTE["gdiff"])
            nc.scalar.activation(e_k[:].rearrange("p t h -> p (t h)"), gdiff[:], ACT.Exp).then_inc(act_route, 1)
            nc.scalar.activation(e_q[:].rearrange("p t h -> p (t h)"), gc[:].rearrange("p t h -> p (t h)"), ACT.Exp).then_inc(act_route, 1)

            def copy_qk(i, j):
                s = i * 2 + j
                act.wait_ge(qk_ready, s + 1)
                if not (isinstance(i, int) and s == 0):
                    act.wait_ge(a_ready, s * 2)
                for h in range(H):
                    r = slice(h * DK, (h + 1) * DK)
                    nc.scalar.activation(qb[r, :, h, :], psQK[r, 0:SEQ].rearrange("p (k t) -> p k t", k=2), ACT.Copy, scale=float(DK) ** -0.5)
                if not (isinstance(i, int) and s < 2):
                    act.wait_ge(inter_ready, s - 1)
                nc.scalar.activation(qT1[j][:], psQK[:, P:SEQ], ACT.Copy, scale=float(DK) ** -0.5)
                nc.scalar.copy(kT[:], psQK[:, SEQ:2 * SEQ]).then_inc(qk_copied, 1)

            def tanh(i, j):
                s = i * 2 + j
                act.wait_ge(vg_ready, s + 1)
                if not (isinstance(i, int) and s == 0):
                    act.wait_ge(gate_ready, s)
                nc.scalar.activation(th[:], psVG[:, :, HV:2 * HV], ACT.Tanh, scale=0.5)

            def copy_v(i, j):
                s = i * 2 + j
                if not (isinstance(i, int) and s < 2):
                    act.wait_ge(o_ready, s - 1)
                nc.scalar.copy(v_sb[j][:], psVG[:, :, 0:HV]).then_inc(v_copied, 1)

            def exp_dec(i, j):
                s = i * 2 + j
                act.wait_ge(pool_dec, (s + 1) * 2)
                if not (isinstance(i, int) and s < 2):
                    act.wait_ge(p_ready, (s - 1) * 2)
                nc.scalar.activation(E[j][:].rearrange("p k n -> p (k n)"), gcB[j][:].rearrange("p h t -> p (h t)"), ACT.Exp).then_inc(e_ready, 1)

            def copy_o(i, j):
                s = i * 2 + j
                act.wait_ge(o_ready, s + 1)
                if not (isinstance(i, int) and s == 0):
                    act.wait_ge(dve_on, (s - 1) * ON_N + 1)
                nc.scalar.copy(oo[:].rearrange("p k n -> p (k n)"), psO[:]).then_inc(o_copied, 1)

            def copy_oT(i, j):
                s = i * 2 + j
                act.wait_ge(oT_ps_ready, s + 1)
                if not (isinstance(i, int) and s == 0):
                    act.wait_ge(wo_ready, s)
                nc.scalar.copy(oT[:].rearrange("p a t -> p (a t)"), psT[:]).then_inc(oT_copied, 1)

            act.wait_ge(pool_consts, POOL_CONSTS)
            copy_qk(0, 0)
            tanh(0, 0)
            copy_v(0, 0)
            exp_dec(0, 0)
            copy_qk(0, 1)
            tanh(0, 1)
            copy_v(0, 1)

            def step(i, j):
                copy_o(i, j)
                exp_dec(*turn(i, j, 1, 2))
                copy_qk(*turn(i, j, 2, 2))
                tanh(*turn(i, j, 2, 2))
                copy_v(*turn(i, j, 2, 2))
                copy_oT(i, j)

            step(0, 0)
            step(0, 1)
            with act.Fori(1, SEQS // 2 - 1) as i:
                for j in range(2):
                    step(i, j)
            last = SEQS // 2 - 1
            copy_o(last, 0)
            exp_dec(last, 1)
            copy_oT(last, 0)
            copy_o(last, 1)
            copy_oT(last, 1)

            psXT = [psQK, psKS]

            def copy_rows(i, j):
                b = i * 4 + j
                act.wait_ge(xgT_ps_ready, b + 1)
                if not (isinstance(i, int) and b < 2):
                    act.wait_ge(h_ready, b - 1)
                nc.scalar.copy(xgT[j % 2][:], psXT[j % 2][:, 0:P]).then_inc(xgT_copied, 1)

            def gelu(i, j):
                b = i * 4 + j
                act.wait_ge(h_ready, b + 1)
                if not (isinstance(i, int) and b < 2):
                    act.wait_ge(y_ready, b - 1)
                for c in range(FC):
                    last = nc.scalar.activation(hid[j % 2][:, c, :], psVG[:, j % 2, c * P:(c + 1) * P], ACT.Gelu,
                                                bias=wbuf[j % 2][:, FF + c:FF + c + 1])
                last.then_inc(gelu_done, 1)

            copy_rows(0, 0)
            for j in range(4):
                if j < 3:
                    copy_rows(0, j + 1)
                else:
                    copy_rows(1, 0)
                gelu(0, j)
            with act.Fori(1, BLOCKS // 4 - 1) as i:
                for j in range(4):
                    copy_rows(*turn(i, j, 1, 4))
                    gelu(i, j)
            last = BLOCKS // 4 - 1
            for j in range(4):
                if j < 3:
                    copy_rows(last, j + 1)
                gelu(last, j)

        @block.vector
        def _(dve):
            c_stats = Chain(dve, dve_stats, STATS_N)
            c_max = Chain(dve, dve_max, MAX_N)
            c_weight = Chain(dve, dve_weight, WEIGHT_N)

            def statistics(i, q):
                g = i * 4 + q
                c_stats.begin(g)
                dve.wait_ge(x_loaded[q], (i + 1) * 16)
                for k in range(GT):
                    c_stats.up(nc.vector.bn_stats(stats[q][:, k, :], x_all[:, bass.ds(g * GT + k, 1), :].rearrange("p a d -> p (a d)")))
                c_stats.wait()
                dve.sem_inc(tick, 1)
                for k in range(GT):
                    c_stats.up(nc.vector.bn_aggr(mv[q][:, k, :], stats[q][:, k, :]))
                c_stats.wait()
                c_stats.up(nc.vector.tensor_scalar(vpe[q][:], mv[q][:, :, 1], LN_EPS, None, ALU.add))
                c_stats.end()

            def mean_term(i, q):
                g = i * 4 + q
                if not (isinstance(i, int) and i == 0):
                    dve.wait_ge(xn_ready, g - 3)
                dve.wait_ge(rstd_ready, g + 1)
                nc.vector.scalar_tensor_tensor(nmr[q][:], mv[q][:, :, 0], -1.0, rstd[q][:], ALU.mult, ALU.mult).then_inc(nmr_ready, 1)

            def logit_max(i, q):
                g = i * 4 + q
                c_max.begin(g)
                dve.wait_ge(lg_ready, g + 1)
                rows = psVG[:, q % 2, 0:GT * NL].rearrange("p (k n) -> p k n", n=NL)
                c_max.up(nc.vector.tensor_reduce(lmax[q][:], rows[:, :, 0:EXP], AX.X, ALU.max))
                c_max.up(nc.vector.tensor_copy(lg_all[:, bass.ds(g * GT, GT), :], rows))
                c_max.wait()
                c_max.up(nc.vector.tensor_tensor(d_all[:, bass.ds(g * GT, GT), :], rows[:, :, 0:EXP],
                                                 lmax[q][:].unsqueeze(2).to_broadcast([P, GT, EXP]), ALU.subtract))
                c_max.end()

            def weight(i, q):
                g = i * 4 + q
                c_weight.begin(g)
                dve.wait_ge(ex_ready, g + 1)
                c_weight.up(nc.vector.tensor_reduce(sumex[q][:], ex[q][:], AX.X, ALU.add))
                c_weight.wait()
                c_weight.up(nc.vector.reciprocal(xw[q][:, :, D], sumex[q][:]))
                c_weight.end()

            dve.wait_ge(pool_consts, POOL_CONSTS)
            def norm_step(i, q):
                if not (isinstance(i, int) and i * 4 + q + 1 >= GROUPS):
                    statistics(*turn(i, q, 1, 4))
                mean_term(i, q)
                if not (isinstance(i, int) and i * 4 + q < 2):
                    logit_max(*turn(i, q, -2, 4))
                if not (isinstance(i, int) and i * 4 + q < 3):
                    weight(*turn(i, q, -3, 4))

            statistics(0, 0)
            for q in range(4):
                norm_step(0, q)
            with dve.Fori(1, GROUPS // 4 - 1) as i:
                for q in range(4):
                    norm_step(i, q)
            last = GROUPS // 4 - 1
            for q in range(4):
                norm_step(last, q)
            logit_max(last, 2)
            weight(last, 1)
            logit_max(last, 3)
            weight(last, 2)
            weight(last, 3)

            c = Chain(dve, dve_route, 0)
            c.begin(0)

            def then(ins, name=None):
                c.up(ins)
                if name:
                    assert ROUTE[name] == c.n, (name, c.n)
                c.wait()

            def bc(ap, shape):
                return ap.to_broadcast(shape)

            dve.wait_ge(dve_max, GROUPS * MAX_N)
            dve.wait_ge(small_loaded, SMALL * 16)
            then(nc.vector.tensor_tensor(z[:], lg_all[:, :, EXP:NL], bc(bgk_bc[:].unsqueeze(1), [P, TILES, H]), ALU.add))
            zf = z[:].rearrange("p t h -> p (t h)")
            then(nc.vector.scalar_tensor_tensor(az[:], zf, -1.0, zf, ALU.mult, ALU.max), "az")
            then(nc.vector.tensor_copy(rev[:], rev_i[:]))
            then(nc.vector.scalar_tensor_tensor(val[:], d_all[:], 0.0, bc(rev[:].unsqueeze(1), [P, TILES, EXP]), ALU.is_equal, ALU.mult))
            then(nc.vector.tensor_reduce(vmax[:], val[:], AX.X, ALU.max))
            then(nc.vector.tensor_tensor(onehot[:], val[:], bc(vmax[:].unsqueeze(2), [P, TILES, EXP]), ALU.is_equal), "onehot")
            dve.wait_ge(act_route, 2)
            then(nc.vector.scalar_tensor_tensor(g_all[:], zf, 0.0, l1[:], ALU.min, ALU.subtract))
            then(nc.vector.tensor_scalar(g_all[:], g_all[:], 1.0 / GATE_NORM, None, ALU.mult), "g")
            dve.wait_ge(pe_route, 1)
            gcf = gc[:].rearrange("p t h -> p (t h)")
            then(nc.vector.tensor_copy(gcf, psQK[:, 0:TH]), "gc")
            then(nc.vector.tensor_tensor(gdiff[:], psQK[:, TH:2 * TH], gcf, ALU.subtract), "gdiff")
            dve.wait_ge(pe_route, 2)
            then(nc.vector.tensor_copy(pre[0][:, PAD:], psT[:, 0:TE]))
            k, a = EXP, 0
            while k < TE:
                then(nc.vector.tensor_tensor(pre[1 - a][:, PAD:], pre[a][:, PAD:], pre[a][:, PAD - k:PAD + TE - k], ALU.add))
                k, a = 2 * k, 1 - a
            total = pre[a][:, PAD + TE - EXP:]
            earlier = pre[a][:, PAD - EXP:PAD + TE - EXP].rearrange("p (t e) -> p t e", e=EXP)
            then(nc.vector.tensor_scalar(tot_i[:], total, float(P - 1), None, ALU.add))
            then(nc.vector.tensor_scalar(nb_i[:], tot_i[:], P.bit_length() - 1, None, ALU.arith_shift_right))
            then(nc.vector.tensor_copy(cb[0][:, EXP:], nb_i[:]))
            k, a = 1, 0
            while k < EXP:
                then(nc.vector.tensor_tensor(cb[1 - a][:, EXP:], cb[a][:, EXP:], cb[a][:, EXP - k:2 * EXP - k], ALU.add))
                k, a = 2 * k, 1 - a
            upto_e = cb[a][:, EXP:]
            then(nc.vector.tensor_scalar(base[:], cb[a][:, EXP - 1:2 * EXP - 1], float(P), None, ALU.mult))
            then(nc.vector.tensor_tensor(slot_f[:], psKS[:, 0:TE].rearrange("p (t e) -> p t e", e=EXP), earlier, ALU.add))
            then(nc.vector.tensor_tensor(slot_f[:], slot_f[:], bc(base[:].unsqueeze(1), [P, TILES, EXP]), ALU.add))
            then(nc.vector.tensor_tensor(slot_f[:], slot_f[:], onehot[:], ALU.mult))
            then(nc.vector.tensor_reduce(pos[:], slot_f[:], AX.X, ALU.add))
            then(nc.vector.tensor_copy(pos_i[:], pos[:]))
            then(nc.vector.tensor_scalar(lo_i[:], pos_i[:], P - 1, None, ALU.bitwise_and))
            then(nc.vector.tensor_scalar(hi_i[:], pos_i[:], P.bit_length() - 1, None, ALU.arith_shift_right))
            then(nc.vector.tensor_copy(lo[:], lo_i[:]))
            then(nc.vector.tensor_copy(hi[:], hi_i[:]))
            then(nc.vector.tensor_copy(iota_f[:], iota_i[:]))
            then(nc.vector.tensor_copy(part1[:], part_i[:]))
            then(nc.vector.tensor_tensor(row1h, bc(iota_f[:].unsqueeze(1), [P, TILES, P]), bc(lo[:].unsqueeze(2), [P, TILES, P]), ALU.is_equal))
            then(nc.vector.tensor_tensor(blk1h, bc(iota_f[:, 0:BLOCKS].unsqueeze(1), [P, TILES, BLOCKS]),
                                         bc(hi[:].unsqueeze(2), [P, TILES, BLOCKS]), ALU.is_equal))
            then(nc.vector.tensor_scalar(blkval[:, :, 0, :], blk1h, part1[:, 0:1], None, ALU.mult))
            then(nc.vector.tensor_tensor(blkval[:, :, 1, :], blk1h, bc(iota_f[:, 0:TILES].unsqueeze(2), [P, TILES, BLOCKS]), ALU.mult), "blkval")
            dve.wait_ge(pe_route, 3)
            then(nc.vector.tensor_copy(gcT[:].rearrange("p a t -> p (a t)"), psO[:, 0:2 * P]), "gcT")
            then(nc.vector.tensor_copy(w1b[:, :, FF:WB], psO[:, 2 * P:2 * P + EXP * FC].rearrange("p (e c) -> p e c", c=FC)))
            dve.wait_ge(proj_loaded, 16 * 5)
            for a in range(2):
                then(nc.vector.tensor_scalar(wo_sb[:, a, :], wo_raw[:, a, :], gn_col[:, 0:1], 0.5, ALU.mult, ALU.mult))
            then(nc.vector.tensor_tensor(isge[:], bc(iota_f[:, 0:BLOCKS].unsqueeze(2), [P, BLOCKS, EXP - 1]),
                                         bc(upto_e[:, 0:EXP - 1].unsqueeze(1), [P, BLOCKS, EXP - 1]), ALU.is_ge))
            then(nc.vector.tensor_reduce(be_f[:], isge[:], AX.X, ALU.add))
            then(nc.vector.tensor_copy(be[:], be_f[:]))
            dve.wait_ge(pe_route, 4)
            then(nc.vector.tensor_copy(part1_of[:], psA[:, 1, 0:BLOCKS]))
            then(nc.vector.scalar_tensor_tensor(id1[:], psA[:, 1, BLOCKS:2 * BLOCKS], float(P), part1_of[:], ALU.mult, ALU.add))
            then(nc.vector.tensor_scalar(gid[:], id1[:], -1.0, 0.0, ALU.add, ALU.max))
            then(nc.vector.tensor_scalar(empty[:], part1_of[:], 0.0, 2.0 * TOKENS, ALU.is_equal, ALU.mult))
            then(nc.vector.scalar_tensor_tensor(sid[:], id1[:], -1.0, empty[:], ALU.add, ALU.add), "all")
            dve.wait_ge(act_route, 4)

            c_comb = Chain(dve, dve_comb, COMB_N)
            c_on = Chain(dve, dve_on, ON_N)

            def combine(i, j):
                s = i * 2 + j
                c_comb.begin(s)
                dve.wait_ge(inter_ready, s + 1)
                c_comb.up(nc.vector.tensor_tensor(inter[:].rearrange("p (h d) -> p h d", d=DV), psKS[:, 0:HV].rearrange("p (h d) -> p h d", d=DV),
                                                  bc(e_q[:, bass.ds(s * 2 + 1, 1), :].rearrange("p a h -> p (a h)").unsqueeze(2), [P, H, DV]), ALU.mult))
                c_comb.wait()
                dve.wait_ge(o_copied, s + 1)
                c_comb.up(nc.vector.tensor_tensor(oo[:, 1, :], inter[:], oo[:, 1, :], ALU.add))
                c_comb.wait()
                c_comb.up(nc.vector.tensor_tensor(sq[:], oo[:], oo[:], ALU.mult))
                c_comb.wait()
                c_comb.up(nc.vector.tensor_reduce(ms[:], sq[:].rearrange("p k (h d) -> p (k h) d", d=DV), AX.X, ALU.add))
                c_comb.wait()
                c_comb.up(nc.vector.tensor_scalar(msn[:], ms[:], 1.0 / DV, RMS_EPS, ALU.mult, ALU.add))
                c_comb.end()

            def probs(i, j):
                s = i * 2 + j
                dve.wait_ge(e_ready, s + 1)
                if not (isinstance(i, int) and s == 0):
                    dve.wait_ge(o_ready, s)
                for k in range(2):
                    dve.wait_ge(a_ready, s * 2 + k + 1)
                    nc.vector.tensor_tensor(pr[:, k, :], psA[:, k, :], E[j][:, k, :], ALU.mult).then_inc(p_ready, 1)

            def decay_k(i, j):
                s = i * 2 + j
                dve.wait_ge(k0_ready, s + 1)
                nc.vector.tensor_tensor(kd[:].rearrange("p (h d) -> p h d", d=DK), psKS[:, 0:P].rearrange("p (h d) -> p h d", d=DK),
                                        bc(e_k[:, bass.ds(s * 2, 1), :].rearrange("p a h -> p (a h)").unsqueeze(2), [P, H, DK]), ALU.mult).then_inc(kd_ready, 1)

            def normed(i, j):
                s = i * 2 + j
                c_on.begin(s)
                c_on.up(nc.vector.tensor_tensor(og[:], oo[:], gate[j][:], ALU.mult))
                c_on.wait()
                dve.wait_ge(rms_ready, s + 1)
                if not (isinstance(i, int) and s == 0):
                    dve.wait_ge(oT_ps_ready, s)
                c_on.up(nc.vector.tensor_tensor(on[:].rearrange("p k (h d) -> p (k h) d", d=DV), og[:].rearrange("p k (h d) -> p (k h) d", d=DV),
                                                bc(rms[:].unsqueeze(2), [P, 2 * H, DV]), ALU.mult))
                c_on.end()

            def copy_state(i, j):
                s = i * 2 + j
                dve.wait_ge(s_ready, s + 1)
                if not (isinstance(i, int) and s == 0):
                    dve.wait_ge(inter_ready, s)
                nc.vector.tensor_tensor(S_sb[:], psKS[:, HV:2 * HV], headmask[:], ALU.mult).then_inc(s_copied, 1)

            def make_gate(i, j):
                s = i * 2 + j
                dve.wait_ge(v_copied, s + 1)
                nc.vector.scalar_tensor_tensor(gate[j][:], th[:], 1.0, psVG[:, :, HV:2 * HV], ALU.add, ALU.mult).then_inc(gate_ready, 1)

            def residual(i, j):
                s = i * 2 + j
                dve.wait_ge(wo_ready, s + 1)
                if not (isinstance(i, int) and s < 2):
                    dve.wait_ge(res_stored[j], i * 16)
                nc.vector.tensor_tensor(res[j][:], psT[:, 0:2 * D].rearrange("p (k d) -> p k d", d=D), x_all[:, bass.ds(s * 2, 2), :],
                                        ALU.add).then_inc(res_ready, 1)

            make_gate(0, 0)
            probs(0, 0)
            decay_k(0, 0)
            copy_state(0, 0)
            make_gate(0, 1)
            combine(0, 0)
            probs(0, 1)
            decay_k(0, 1)
            normed(0, 0)
            copy_state(0, 1)
            make_gate(1, 0)
            with dve.Fori(1, SEQS // 2 - 1) as i:
                for j in range(2):
                    pi, pj = turn(i, j, -1, 2)
                    ni, nj = turn(i, j, 1, 2)
                    combine(pi, pj)
                    probs(i, j)
                    decay_k(i, j)
                    normed(pi, pj)
                    copy_state(i, j)
                    make_gate(ni, nj)
                    residual(i - 1, j)
            last = SEQS // 2 - 1
            combine(last - 1, 1)
            probs(last, 0)
            decay_k(last, 0)
            normed(last - 1, 1)
            copy_state(last, 0)
            make_gate(last, 1)
            residual(last - 1, 0)
            combine(last, 0)
            probs(last, 1)
            decay_k(last, 1)
            normed(last, 0)
            copy_state(last, 1)
            residual(last - 1, 1)
            combine(last, 1)
            normed(last, 1)
            residual(last, 0)
            residual(last, 1)

            c_y = Chain(dve, dve_y, Y_N)
            psY = [psO, psT]

            def copy_gidx(i, j):
                b = i * 4 + j
                if not (isinstance(i, int) and i == 0):
                    dve.wait_ge(gathered[j], i * 16)
                nc.vector.tensor_copy(gidx[j][:], gid[:, bass.ds(b, 1)]).then_inc(gidx_ready, 1)

            def copy_w(i, j):
                b = i * 4 + j
                e = dve.value_load(be[0:1, bass.ds(b, 1)], min_val=0, max_val=EXP - 1)
                if not (isinstance(i, int) and b < 2):
                    dve.wait_ge(gelu_done, b - 1)
                nc.vector.tensor_copy(wbuf[j % 2], w1b[:, bass.ds(e, 1), :].rearrange("p a n -> p (a n)")).then_inc(w_copied, 1)

            def weigh(i, j):
                b = i * 4 + j
                c_y.begin(b)
                e = dve.value_load(be[0:1, bass.ds(b, 1)], min_val=0, max_val=EXP - 1)
                if not (isinstance(i, int) and i == 0):
                    dve.wait_ge(scattered[j], i * 16)
                nc.vector.tensor_copy(sidx[j][:], sid[:, bass.ds(b, 1)]).then_inc(sidx_ready, 1)
                dve.wait_ge(y_ready, b + 1)
                c_y.up(nc.vector.tensor_tensor(yb[j % 2][:], psY[j % 2][:, 0:D], b2_bc[:, bass.ds(e, 1), :].rearrange("p a d -> p (a d)"), ALU.add))
                c_y.wait()
                dve.wait_ge(gathered[j], (i + 1) * 16)
                c_y.up(nc.vector.tensor_scalar(yw[j][:], yb[j % 2][:], xg[j][:, D:D + 1], None, ALU.mult))
                c_y.end()

            dve.wait_ge(expert_loaded, 2 * 16)
            dve.wait_ge(w_loaded, (EXP + 1) * 16)
            for j in range(4):
                copy_gidx(0, j)
            copy_w(0, 0)
            copy_w(0, 1)

            def expert_step(i, j, blocks_left):
                if blocks_left > 2:
                    copy_w(*turn(i, j, 2, 4))
                if blocks_left > 4:
                    copy_gidx(i + 1, j)
                weigh(i, j)

            for j in range(4):
                expert_step(0, j, BLOCKS)
            with dve.Fori(1, BLOCKS // 4 - 1) as i:
                for j in range(4):
                    expert_step(i, j, BLOCKS)
            for j in range(4):
                expert_step(BLOCKS // 4 - 1, j, 4 - j)


POOL_CONSTS = 22
SMALL = 5
ROUTE = {"az": 2, "onehot": 6, "g": 8, "gc": 9, "gdiff": 10, "blkval": 39, "gcT": 40, "all": 51}


_INS = ["L0_attn_x", "L0_attn_Wq", "L0_attn_Wk", "L0_attn_Wv", "L0_attn_Wg", "L0_attn_Wgk", "L0_attn_bgk", "L0_attn_Wo",
        "L0_attn_gnorm_w", "L0_ffn_gate_w", "L0_ffn_w1", "L0_ffn_b1", "L0_ffn_w2", "L0_ffn_b2"]


def kernel(**inputs):
    import numpy as _np
    import concourse.bacc as _bacc
    from concourse import mybir as _mybir
    from concourse.bass_utils import run_bass_kernel_spmd as _run

    nc = _bacc.Bacc("TRN2", target_bir_lowering=False, num_devices=1)
    arrays, args = {}, []
    for name in _INS:
        a = _np.ascontiguousarray(inputs[name])
        arrays[f"in_{name}_dram"] = a
        args.append(nc.dram_tensor(f"in_{name}_dram", a.shape, _mybir.dt.from_np(a.dtype), kind="ExternalInput").ap())
    shape = inputs["L0_attn_x"].shape
    args.append(nc.dram_tensor("out_0_dram", shape, _mybir.dt.float32, kind="ExternalOutput").ap())
    build_layer(nc, *args)
    r = _run(nc, [arrays], core_ids=[0])
    return r.results[0]["out_0_dram"]
```

```python
from contextlib import ExitStack

import concourse.bass as bass
from concourse import mybir

ALU = mybir.AluOpType
ACT = mybir.ActivationFunctionType
AX = mybir.AxisListType
F32 = mybir.dt.float32
BF16 = mybir.dt.bfloat16
I32 = mybir.dt.int32

P = 128
LN_EPS = 1e-5
RMS_EPS = 1e-5
GATE_NORM = 16.0
MASKED = -1e30


def turn(i, j, d, n):
    return i + (j + d) // n, (j + d) % n


class Chain:

    def __init__(self, eng, sem, per_step):
        self.eng, self.sem, self.per_step = eng, sem, per_step

    def begin(self, step):
        self.base, self.n = step * self.per_step, 0

    def up(self, ins):
        ins.then_inc(self.sem, 1)
        self.n += 1

    def wait(self):
        self.eng.wait_ge(self.sem, self.base + self.n)

    def end(self):
        assert self.n == self.per_step


def build_layer(nc, x, Wq, Wk, Wv, Wg, Wgk, bgk, Wo, gnorm_w, gate_w, w1, b1, w2, b2, out):
    SEQS, SEQ, D = x.shape
    TOKENS = SEQS * SEQ
    TILES = TOKENS // P
    H = Wgk.shape[1]
    DK = Wq.shape[1] // H
    DV = Wv.shape[1] // H
    HV = H * DV
    EXP, _, FF = w1.shape
    FC = FF // P
    NL = EXP + H
    assert D == P and H * DK == P and SEQ == 2 * P and HV == 2 * P and FF == 4 * P

    GT = 4
    GROUPS = TILES // GT
    R = 6
    BLOCKS = -(-(TILES + EXP - 1) // R) * R
    XW = D + 1
    WB = FF + FC + D
    PAD = TILES // 2 * EXP
    TE = TILES * EXP
    TH = TILES * H

    x_t = x.rearrange("s (k p) d -> p (s k) d", p=P)
    x_rows = x_t
    out_rows = out.rearrange("s n d -> (s n) d")
    out_t = out.rearrange("s (k p) d -> p (s k) d", p=P)
    xw_dram = nc.dram_tensor("xn_and_weight", [TOKENS, XW], F32).ap()
    xw_t = xw_dram.rearrange("(t p) c -> p t c", p=P)
    xt_dram = nc.dram_tensor("xn_transposed", [GROUPS, P, GT * P], F32).ap()
    table_dram = nc.dram_tensor("sorted_table", [P * BLOCKS, 1], I32).ap()
    gc_dram = nc.dram_tensor("decay_rows", [TH, P], F32).ap()

    with ExitStack() as ctx:
        def sb(name, shape, dt=F32):
            return ctx.enter_context(nc.sbuf_tensor(name, shape, dt))

        def ps(name, shape):
            return ctx.enter_context(nc.psum_tensor(name, shape, F32))

        def sem(name):
            return ctx.enter_context(nc.semaphore(name))

        ident = sb("ident", [P, P])
        upto = sb("upto", [P, P])
        onesf = sb("onesf", [P, P])
        before = sb("before", [P, P], BF16)
        onesb = sb("onesb", [P, P], BF16)
        iota_i = sb("iota_i", [P, P], I32)
        iota_f = sb("iota_f", [P, P])
        ids = sb("ids", [P, TILES], I32)
        rev_i = sb("rev_i", [P, EXP], I32)
        rev = sb("rev", [P, EXP])
        neg_half = sb("neg_half", [P, 8])
        headmask = sb("headmask", [P, HV])
        wq_sb = sb("wq_sb", [P, H * DK])
        wk_sb = sb("wk_sb", [P, H * DK])
        wvg_sb = sb("wvg_sb", [P, 2 * HV])
        wr_sb = sb("wr_sb", [P, NL])
        wo_raw = sb("wo_raw", [P, 2, D])
        wo_sb = sb("wo_sb", [P, 2, D])
        gn_col = sb("gn_col", [P, 1])
        bgk_bc = sb("bgk_bc", [P, H])
        b1_rows = sb("b1_rows", [EXP * FC, P])
        w1b = sb("w1b", [P, EXP, WB])
        w2_sb = sb("w2_sb", [P, EXP, FC, D])

        x_all = sb("x_all", [P, TILES, D])
        stats = [sb(f"stats{q}", [P, GT, 6]) for q in range(4)]
        mv = [sb(f"mv{q}", [P, GT, 2]) for q in range(4)]
        vpe = [sb(f"vpe{q}", [P, GT]) for q in range(4)]
        rstd = [sb(f"rstd{q}", [P, GT]) for q in range(4)]
        nmr = [sb(f"nmr{q}", [P, GT]) for q in range(4)]
        xw = [sb(f"xw{q}", [P, GT, XW]) for q in range(4)]
        xts = [sb(f"xts{q}", [P, GT * P]) for q in range(2)]
        lg_all = sb("lg_all", [P, TILES, NL])
        lmax = [sb(f"lmax{q}", [P, GT]) for q in range(4)]
        d_all = sb("d_all", [P, TILES, EXP])
        ex = [sb(f"ex{q}", [P, GT, EXP]) for q in range(4)]
        sumex = [sb(f"sumex{q}", [P, GT]) for q in range(4)]

        z = sb("z", [P, TILES, H])
        az = sb("az", [P, TH])
        ez = sb("ez", [P, TH])
        l1 = sb("l1", [P, TH])
        g_all = sb("g_all", [P, TH])
        gc = sb("gc", [P, TILES, H])
        gdiff = sb("gdiff", [P, TH])
        e_k = sb("e_k", [P, TILES, H])
        e_q = sb("e_q", [P, TILES, H])
        gcT = sb("gcT", [P, 2, P])
        val = sb("val", [P, TILES, EXP])
        vmax = sb("vmax", [P, TILES])
        onehot = sb("onehot", [P, TILES, EXP], BF16)
        pre = [sb(f"pre{q}", [P, PAD + TE]) for q in range(2)]
        tot_i = sb("tot_i", [P, EXP], I32)
        nb_i = sb("nb_i", [P, EXP], I32)
        cb = [sb(f"cb{q}", [P, 2 * EXP]) for q in range(2)]
        base = sb("base", [P, EXP])
        slot_f = sb("slot_f", [P, TILES, EXP])
        pos = sb("pos", [P, TILES])
        pos_i = sb("pos_i", [P, TILES], I32)
        lo_i = sb("lo_i", [P, TILES], I32)
        hi_i = sb("hi_i", [P, TILES], I32)
        place = sb("place", [P, TILES, 2], I32)
        place_s = [sb(f"place{j}", [P, 2, 2], I32) for j in range(2)]
        none = sb("none", [P, BLOCKS], I32)
        sid = sb("sid", [P, BLOCKS], I32)
        gid = sb("gid", [P, BLOCKS], I32)
        isge = sb("isge", [P, BLOCKS, EXP - 1])
        be_f = sb("be_f", [P, BLOCKS])
        be = sb("be", [P, BLOCKS], I32)

        xT = [sb(f"xT{j}", [P, SEQ]) for j in range(2)]
        gcB = [sb(f"gcB{j}", [P, 2 * H, P]) for j in range(2)]
        E = [sb(f"E{j}", [P, 2, H * P]) for j in range(2)]
        qb = sb("qb", [P, 2, H, P])
        qT1 = [sb(f"qT1{j}", [P, P]) for j in range(2)]
        kT = sb("kT", [P, SEQ])
        v_sb = [sb(f"v_sb{j}", [P, 2, HV]) for j in range(2)]
        th = sb("th", [P, 2, HV])
        gate = [sb(f"gate{j}", [P, 2, HV]) for j in range(2)]
        kd = sb("kd", [P, H * DK])
        S_sb = sb("S_sb", [P, HV])
        pr = sb("pr", [P, 2, H * P])
        inter = sb("inter", [P, HV])
        oo = sb("oo", [P, 2, HV])
        sq = sb("sq", [P, 2, HV])
        ms = sb("ms", [P, 2 * H])
        msn = sb("msn", [P, 2 * H])
        rms = sb("rms", [P, 2 * H])
        og = sb("og", [P, 2, HV])
        on = sb("on", [P, 2, HV])
        oT = sb("oT", [P, 4, P])
        res = [sb(f"res{j}", [P, 2, D]) for j in range(2)]

        gidx = [sb(f"gidx{j}", [P, 1], I32) for j in range(R)]
        sidx = [sb(f"sidx{j}", [P, 1], I32) for j in range(R)]
        xg = [sb(f"xg{j}", [P, XW]) for j in range(R)]
        xgT = [sb(f"xgT{j}", [P, P]) for j in range(2)]
        wbuf = [t[:].rearrange("p k n -> p (k n)")[:, 0:WB] for t in (E[0], E[1], gcB[0])]
        hid = [t[:].rearrange("p k (c n) -> p (k c) n", n=P) for t in (sq, og)]
        yb = [sb(f"yb{j}", [P, D]) for j in range(2)]
        yw = [sb(f"yw{j}", [P, D]) for j in range(R)]

        psQK = ps("psQK", [P, 512])
        psVG = ps("psVG", [P, 2, 512])
        psKS = ps("psKS", [P, 512])
        psA = ps("psA", [P, 2, 512])
        psO = ps("psO", [P, 512])
        psT = ps("psT", [P, 512])

        x_loaded = [sem(f"x_loaded{q}") for q in range(4)]
        small_loaded = sem("small_loaded")
        proj_loaded = sem("proj_loaded")
        w_loaded = sem("w_loaded")
        xw_stored = [sem(f"xw_stored{q}") for q in range(4)]
        xt_stored = [sem(f"xt_stored{q}") for q in range(2)]
        gc_stored = sem("gc_stored")
        xT_loaded = [sem(f"xT_loaded{j}") for j in range(2)]
        gcB_loaded = [sem(f"gcB_loaded{j}") for j in range(2)]
        res_stored = [sem(f"res_stored{j}") for j in range(2)]
        gathered = [sem(f"gathered{j}") for j in range(R)]
        scattered = [sem(f"scattered{j}") for j in range(R)]
        pool_consts = sem("pool_consts")
        consts = sem("consts")
        dve_stats = sem("dve_stats")
        rstd_ready = sem("rstd_ready")
        nmr_ready = sem("nmr_ready")
        xn_ready = sem("xn_ready")
        xt_ps_ready = sem("xt_ps_ready")
        xts_ready = sem("xts_ready")
        lg_ready = sem("lg_ready")
        dve_max = sem("dve_max")
        ex_ready = sem("ex_ready")
        dve_weight = sem("dve_weight")
        dve_route = sem("dve_route")
        act_route = sem("act_route")
        pe_route = sem("pe_route")
        none_ready = sem("none_ready")
        table_cleared = sem("table_cleared")
        place_ready = sem("place_ready")
        placed = [sem(f"placed{j}") for j in range(2)]
        table_loaded = sem("table_loaded")
        gid_ready = sem("gid_ready")
        qk_ready = sem("qk_ready")
        vg_ready = sem("vg_ready")
        a_ready = sem("a_ready")
        k0_ready = sem("k0_ready")
        s_ready = sem("s_ready")
        o_ready = sem("o_ready")
        inter_ready = sem("inter_ready")
        oT_ps_ready = sem("oT_ps_ready")
        wo_ready = sem("wo_ready")
        qk_copied = sem("qk_copied")
        v_copied = sem("v_copied")
        o_copied = sem("o_copied")
        e_ready = sem("e_ready")
        oT_copied = sem("oT_copied")
        dve_comb = sem("dve_comb")
        p_ready = sem("p_ready")
        kd_ready = sem("kd_ready")
        dve_on = sem("dve_on")
        s_copied = sem("s_copied")
        gate_ready = sem("gate_ready")
        res_ready = sem("res_ready")
        pool_dec = sem("pool_dec")
        rms_ready = sem("rms_ready")
        tick = sem("tick")
        gidx_ready = sem("gidx_ready")
        sidx_ready = sem("sidx_ready")
        xgT_ps_ready = sem("xgT_ps_ready")
        xgT_copied = sem("xgT_copied")
        w_copied = sem("w_copied")
        h_ready = sem("h_ready")
        gelu_done = sem("gelu_done")
        y_ready = sem("y_ready")
        dve_y = sem("dve_y")

        STATS_N, MAX_N, WEIGHT_N = 9, 3, 2
        COMB_N, ON_N, Y_N = 5, 2, 2
        LAST = SEQS - 1
        FIRST_SEQS = 2

        block = ctx.enter_context(nc.Block())

        @block.sync
        def _(sp):
            def load_x(i, q):
                if not (isinstance(i, int) and i == 0):
                    sp.wait_ge(x_loaded[q], i * 16)
                g = i * 4 + q
                sp.dma_start(x_all[:, bass.ds(g * GT, GT), :], x_t[:, bass.ds(g * GT, GT), :]).then_inc(x_loaded[q], 16)

            def store_xt(i, q):
                g = i * 4 + q
                sp.wait_ge(xts_ready, g + 1)
                sp.dma_start(xt_dram[bass.ds(g, 1), :, :].rearrange("a p n -> p (a n)"), xts[q % 2][:]).then_inc(xt_stored[q % 2], 16)

            def store_xw(i, q):
                g = i * 4 + q
                sp.wait_ge(dve_weight, (g + 1) * WEIGHT_N)
                sp.dma_start(xw_t[:, bass.ds(g * GT, GT), :], xw[q][:]).then_inc(xw_stored[q], 16)

            def norm_step(i, q):
                if not (isinstance(i, int) and i + 1 >= GROUPS // 4):
                    load_x(i + 1, q)
                if not (isinstance(i, int) and i * 4 + q < 1):
                    store_xt(*turn(i, q, -1, 4))
                if not (isinstance(i, int) and i * 4 + q < 3):
                    store_xw(*turn(i, q, -3, 4))

            for q in range(4):
                load_x(0, q)
            sp.wait_ge(none_ready, 1)
            sp.dma_start(table_dram.rearrange("(p b) a -> p (b a)", p=P), none[:]).then_inc(table_cleared, 16)
            for q in range(4):
                norm_step(0, q)
            with sp.Fori(1, GROUPS // 4 - 1) as i:
                for q in range(4):
                    norm_step(i, q)
            for q in range(4):
                norm_step(GROUPS // 4 - 1, q)
            store_xt(GROUPS // 4 - 1, 3)
            for q in range(1, 4):
                store_xw(GROUPS // 4 - 1, q)

            sp.dma_start(w1b[:, :, 0:FF], w1.rearrange("e d f -> d e f")).then_inc(w_loaded, 16)
            sp.dma_start(w1b[:, :, FF + FC:WB], b2.partition_broadcast(P)).then_inc(w_loaded, 16)
            for e in range(EXP):
                sp.dma_start(w2_sb[:, e, :, :], w2[e].rearrange("(c f) d -> f c d", f=P)).then_inc(w_loaded, 16)

            sp.wait_ge(dve_route, ROUTE["gcT"])
            sp.dma_start(gc_dram.rearrange("(a p) t -> p a t", p=P), gcT[:]).then_inc(gc_stored, 16)

            def load_seq(i, j):
                s = i * 2 + j
                sp.dma_start(xT[j][:], xt_dram[bass.ds(i, 1), :, j * SEQ:(j + 1) * SEQ].rearrange("a p n -> p (a n)")).then_inc(xT_loaded[j], 16)
                sp.dma_start(gcB[j][:].rearrange("p h t -> p (h t)"),
                             gc_dram[bass.ds(s * 2 * H, 2 * H), :].rearrange("r t -> (r t)").partition_broadcast(P)).then_inc(gcB_loaded[j], 16)

            def store_res(i, j):
                s = i * 2 + j
                sp.wait_ge(res_ready, s + 1)
                sp.dma_start(out_t[:, bass.ds(s * 2, 2), :], res[j][:]).then_inc(res_stored[j], 16)

            for q in range(4):
                sp.wait_ge(xw_stored[q], GROUPS // 4 * 16)
            for q in range(2):
                sp.wait_ge(xt_stored[q], GROUPS // 2 * 16)
            sp.wait_ge(gc_stored, 16)
            for j in range(2):
                load_seq(0, j)

            def step(i, j):
                s = i * 2 + j
                sp.wait_ge(k0_ready, s + 1)
                sp.wait_ge(e_ready, s + 1)
                load_seq(i + 1, j)

            for j in range(2):
                step(0, j)
            with sp.Fori(1, SEQS // 2 - 1) as i:
                for j in range(2):
                    store_res(i - 1, j)
                    step(i, j)
            for j in range(2):
                sp.wait_ge(placed[j], SEQS // 2 * 32)
            sp.dma_start(sid[:], table_dram.rearrange("(p b) a -> p (b a)", p=P)).then_inc(table_loaded, 16)
            for j in range(2):
                store_res(SEQS // 2 - 2, j)
            for j in range(2):
                store_res(SEQS // 2 - 1, j)
            for j in range(2):
                sp.wait_ge(res_stored[j], SEQS // 2 * 16)
            sp.wait_ge(w_loaded, (EXP + 2) * 16)

        @block.gpsimd
        def _(pool):
            c = [0]

            def const(ins):
                ins.then_inc(pool_consts, 1)
                c[0] += 1

            nc.gpsimd.memset(none[:], TOKENS).then_inc(none_ready, 1)
            const(nc.gpsimd.memset(ident[:], 1.0))
            const(nc.gpsimd.memset(upto[:], 1.0))
            const(nc.gpsimd.memset(onesf[:], 1.0))
            const(nc.gpsimd.memset(before[:], 1.0))
            const(nc.gpsimd.memset(onesb[:], 1.0))
            const(nc.gpsimd.memset(neg_half[:], -0.5))
            const(nc.gpsimd.memset(headmask[:], 0.0))
            const(nc.gpsimd.memset(qb[:], 0.0))
            for q in range(2):
                const(nc.gpsimd.memset(pre[q][:, 0:PAD], 0.0))
                const(nc.gpsimd.memset(cb[q][:, 0:EXP], 0.0))
            const(nc.gpsimd.iota(iota_i[:], pattern=[[1, P]], base=0, channel_multiplier=0))
            const(nc.gpsimd.iota(ids[:], pattern=[[P, TILES]], base=0, channel_multiplier=1))
            const(nc.gpsimd.iota(rev_i[:], pattern=[[-1, EXP]], base=EXP, channel_multiplier=0))
            pool.wait_ge(pool_consts, c[0])
            const(nc.gpsimd.affine_select(out=ident[:], in_=ident[:], pattern=[[1, P]], compare_op=ALU.is_equal,
                                          fill=0.0, base=0, channel_multiplier=-1))
            const(nc.gpsimd.affine_select(out=upto[:], in_=upto[:], pattern=[[1, P]], compare_op=ALU.is_ge,
                                          fill=0.0, base=0, channel_multiplier=-1))
            const(nc.gpsimd.affine_select(out=before[:], in_=before[:], pattern=[[1, P]], compare_op=ALU.is_ge,
                                          fill=0.0, base=-1, channel_multiplier=-1))
            for h in range(H):
                pool.wait_ge(pool_consts, c[0])
                const(nc.gpsimd.memset(headmask[h * DK:(h + 1) * DK, h * DV:(h + 1) * DV], 1.0))
            assert c[0] == POOL_CONSTS

            def rstd_step(i, q):
                g = i * 4 + q
                pool.wait_ge(dve_stats, (g + 1) * STATS_N)
                nc.gpsimd.tensor_tensor(rstd[q][:], vpe[q][:], neg_half[:, 0:GT], ALU.pow).then_inc(rstd_ready, 1)

            pool.wait_ge(pool_consts, c[0])
            for q in range(4):
                rstd_step(0, q)
            with pool.Fori(1, GROUPS // 4) as i:
                for q in range(4):
                    pool.wait_ge(xn_ready, i * 4 + q - 3)
                    rstd_step(i, q)

            def dec(i, j):
                s = i * 2 + j
                pool.wait_ge(gcB_loaded[j], (i + 1) * 16)
                nc.gpsimd.tensor_tensor(gcB[j][:], gcB[j][:],
                                        gc[:, bass.ds(s * 2, 2), :].rearrange("p k h -> p (k h)").unsqueeze(2).to_broadcast([P, 2 * H, P]),
                                        ALU.subtract).then_inc(pool_dec, 1)
                pool.wait_ge(pool_dec, s * 2 + 1)
                pool.sem_inc(tick, 1)
                nc.gpsimd.affine_select(out=gcB[j][:], in_=gcB[j][:], pattern=[[0, 2 * H], [1, P]], compare_op=ALU.is_ge,
                                        fill=MASKED, base=0, channel_multiplier=-1).then_inc(pool_dec, 1)

            def rms_step(i, j):
                s = i * 2 + j
                pool.wait_ge(dve_comb, (s + 1) * COMB_N)
                nc.gpsimd.tensor_tensor(rms[:], msn[:], neg_half[:, 0:2 * H], ALU.pow).then_inc(rms_ready, 1)

            def place_ids(i, j):
                s = i * 2 + j
                pool.wait_ge(place_ready, s + 1)
                pool.sem_inc(tick, 1)
                for k in range(2):
                    nc.gpsimd.indirect_dma_start(out=table_dram, out_offset=bass.IndirectOffsetOnAxis(ap=place_s[j][:, k, 0:1], axis=0),
                                                 in_=place_s[j][:, k, 1:2], in_offset=None).then_inc(placed[j], 16)

            def step(i, j):
                pool.wait_ge(dve_on, (i * 2 + j - 1) * ON_N)
                rms_step(*turn(i, j, -1, 2))
                dec(*turn(i, j, 1, 2))
                place_ids(*turn(i, j, 1, 2))

            pool.wait_ge(table_cleared, 16)
            pool.wait_ge(dve_route, ROUTE["gc"])
            dec(0, 0)
            dec(0, 1)
            place_ids(0, 0)
            place_ids(0, 1)
            rms_step(0, 0)
            dec(1, 0)
            place_ids(1, 0)
            with pool.Fori(1, SEQS // 2 - 1) as i:
                for j in range(2):
                    step(i, j)
            last = SEQS // 2 - 1
            pool.wait_ge(dve_on, (LAST - 2) * ON_N)
            rms_step(last - 1, 1)
            dec(last, 1)
            place_ids(last, 1)
            pool.wait_ge(dve_on, (LAST - 1) * ON_N)
            rms_step(last, 0)
            pool.wait_ge(dve_on, LAST * ON_N)
            rms_step(last, 1)

            def gather(i, j):
                b = i * R + j
                pool.wait_ge(gidx_ready, b + 1)
                pool.sem_inc(tick, 1)
                nc.gpsimd.indirect_dma_start(out=xg[j][:], out_offset=None, in_=xw_dram,
                                             in_offset=bass.IndirectOffsetOnAxis(ap=gidx[j][:], axis=0)).then_inc(gathered[j], 16)

            def scatter(i, j):
                b = i * R + j
                pool.wait_ge(dve_y, (b + 1) * Y_N)
                pool.wait_ge(sidx_ready, b + 1)
                pool.sem_inc(tick, 1)
                nc.gpsimd.indirect_dma_start(out=out_rows, out_offset=bass.IndirectOffsetOnAxis(ap=sidx[j][:], axis=0),
                                             in_=yw[j][:], in_offset=None, bounds_check=TOKENS - 1, oob_is_err=False,
                                             compute_op=ALU.add).then_inc(scattered[j], 16)

            for q in range(4):
                pool.wait_ge(xw_stored[q], GROUPS // 4 * 16)
            for j in range(R - 1):
                gather(0, j)
            for j in range(2):
                pool.wait_ge(res_stored[j], SEQS // 2 * 16)

            def step(i, j):
                if not (isinstance(i, int) and i * R + j == 0):
                    pool.wait_ge(dve_y, (i * R + j) * Y_N)
                if not (isinstance(i, int) and i * R + j + R - 1 >= BLOCKS):
                    gather(*turn(i, j, R - 1, R))
                scatter(i, j)

            for j in range(R):
                step(0, j)
            with pool.Fori(1, BLOCKS // R - 1) as i:
                for j in range(R):
                    step(i, j)
            for j in range(R):
                step(BLOCKS // R - 1, j)
            for j in range(R):
                pool.wait_ge(scattered[j], BLOCKS // R * 16)

        @block.tensor
        def _(pe):
            def transposes(i, q):
                g = i * 4 + q
                pe.wait_ge(xn_ready, g + 1)
                if not (isinstance(i, int) and g < 2):
                    pe.wait_ge(xts_ready, g - 1)
                for k in range(GT):
                    last = nc.tensor.transpose(psA[:, q % 2, k * P:(k + 1) * P], xw[q][:, k, 0:D], ident[:])
                last.then_inc(xt_ps_ready, 1)

            def logits(i, q):
                g = i * 4 + q
                pe.wait_ge(xts_ready, g + 1)
                if not (isinstance(i, int) and g < 2):
                    pe.wait_ge(dve_max, (g - 1) * MAX_N)
                for k in range(GT):
                    last = nc.tensor.matmul(psVG[:, q % 2, k * NL:(k + 1) * NL], xts[q % 2][:, k * P:(k + 1) * P], wr_sb[:],
                                            start=True, stop=True)
                last.then_inc(lg_ready, 1)

            pe.wait_ge(pool_consts, POOL_CONSTS)
            pe.wait_ge(small_loaded, SMALL * 16)
            transposes(0, 0)
            for q in range(1, 4):
                logits(0, q - 1)
                transposes(0, q)
            with pe.Fori(1, GROUPS // 4) as i:
                for q in range(4):
                    logits(*turn(i, q, -1, 4))
                    transposes(i, q)
            logits(GROUPS // 4 - 1, 3)

            pe.wait_ge(dve_route, ROUTE["g"])
            nc.tensor.matmul(psQK[:, 0:TH], upto[:], g_all[:], start=True, stop=True)
            nc.tensor.matmul(psQK[:, TH:2 * TH], onesf[:], g_all[:], start=True, stop=True).then_inc(pe_route, 1)
            pe.wait_ge(dve_route, ROUTE["onehot"])
            oh = onehot[:].rearrange("p t e -> p (t e)")
            nc.tensor.matmul(psKS[:, 0:TE], before[:], oh, start=True, stop=True)
            nc.tensor.matmul(psT[:, 0:TE], onesb[:], oh, start=True, stop=True).then_inc(pe_route, 1)
            pe.wait_ge(dve_route, ROUTE["gc"])
            gc_flat = gc[:].rearrange("p t h -> p (t h)")
            for a in range(2):
                nc.tensor.transpose(psO[:, a * P:(a + 1) * P], gc_flat[:, a * P:(a + 1) * P], ident[:])
            nc.tensor.transpose(psO[:, 2 * P:2 * P + EXP * FC], b1_rows[:], ident[0:EXP * FC, 0:EXP * FC]).then_inc(pe_route, 1)
            def proj(i, j):
                s = i * 2 + j
                pe.wait_ge(xT_loaded[j], (i + 1) * 16)
                first = isinstance(i, int) and s == 0
                if not first:
                    pe.wait_ge(qk_copied, s)
                nc.tensor.matmul(psQK[:, 0:SEQ], wq_sb[:], xT[j][:], start=True, stop=True)
                nc.tensor.matmul(psQK[:, SEQ:2 * SEQ], wk_sb[:], xT[j][:], start=True, stop=True).then_inc(qk_ready, 1)
                if not first:
                    pe.wait_ge(v_copied, s)
                    pe.wait_ge(gate_ready, s)
                for k in range(2):
                    last = nc.tensor.matmul(psVG[:, k, :], xT[j][:, k * P:(k + 1) * P], wvg_sb[:], start=True, stop=True)
                last.then_inc(vg_ready, 1)

            def scores(i, j):
                s = i * 2 + j
                pe.wait_ge(qk_copied, s + 1)
                if not (isinstance(i, int) and s == 0):
                    pe.wait_ge(p_ready, s * 2)
                for k in range(2):
                    nc.tensor.matmul(psA[:, k, :], kT[:, k * P:(k + 1) * P], qb[:, k, :, :].rearrange("p h t -> p (h t)"),
                                     start=True, stop=True).then_inc(a_ready, 1)
                if not (isinstance(i, int) and s == 0):
                    pe.wait_ge(dve_comb, (s - 1) * COMB_N + 1)
                nc.tensor.matmul(psKS[:, 0:P], xT[j][:, 0:P], wk_sb[:], start=True, stop=True).then_inc(k0_ready, 1)

            def outputs(i, j):
                s = i * 2 + j
                pe.wait_ge(kd_ready, s + 1)
                pe.wait_ge(v_copied, s + 1)
                nc.tensor.matmul(psKS[:, HV:2 * HV], kd[:], v_sb[j][:, 0, :], start=True, stop=True).then_inc(s_ready, 1)
                if not (isinstance(i, int) and s == 0):
                    pe.wait_ge(o_copied, s)
                for k in range(2):
                    pe.wait_ge(p_ready, s * 2 + k + 1)
                    for h in range(H):
                        last = nc.tensor.matmul(psO[:, k * HV + h * DV:k * HV + (h + 1) * DV], pr[:, k, h * P:(h + 1) * P],
                                                v_sb[j][:, k, h * DV:(h + 1) * DV], start=True, stop=True)
                last.then_inc(o_ready, 1)
                pe.wait_ge(s_copied, s + 1)
                nc.tensor.matmul(psKS[:, 0:HV], qT1[j][:], S_sb[:], start=True, stop=True).then_inc(inter_ready, 1)

            def transpose_on(i, j):
                s = i * 2 + j
                pe.wait_ge(dve_on, (s + 1) * ON_N)
                if not (isinstance(i, int) and s == 0):
                    pe.wait_ge(res_ready, s)
                for k in range(2):
                    for a in range(2):
                        last = nc.tensor.transpose(psT[:, (2 * k + a) * P:(2 * k + a + 1) * P], on[:, k, a * P:(a + 1) * P], ident[:])
                last.then_inc(oT_ps_ready, 1)

            def project_out(i, j):
                s = i * 2 + j
                pe.wait_ge(oT_copied, s + 1)
                for k in range(2):
                    for a in range(2):
                        last = nc.tensor.matmul(psT[:, k * D:(k + 1) * D], oT[:, 2 * k + a, :], wo_sb[:, a, :],
                                                start=(a == 0), stop=(a == 1))
                last.then_inc(wo_ready, 1)

            def step(i, j):
                scores(i, j)
                project_out(*turn(i, j, -2, 2))
                proj(*turn(i, j, 1, 2))
                outputs(i, j)
                transpose_on(*turn(i, j, -1, 2))

            pe.wait_ge(dve_route, ROUTE["all"])
            pe.wait_ge(proj_loaded, 16 * 5)
            proj(0, 0)
            scores(0, 0)
            proj(0, 1)
            outputs(0, 0)
            scores(0, 1)
            proj(1, 0)
            outputs(0, 1)
            transpose_on(0, 0)
            with pe.Fori(1, SEQS // 2 - 1) as i:
                for j in range(2):
                    step(i, j)
            last = SEQS // 2 - 1
            step(last, 0)
            scores(last, 1)
            project_out(last - 1, 1)
            outputs(last, 1)
            transpose_on(last, 0)
            project_out(last, 0)
            transpose_on(last, 1)
            project_out(last, 1)

            psXT = [psQK, psKS]
            psY = [psO, psT]

            def transpose_rows(i, j):
                b = i * R + j
                pe.wait_ge(gathered[j], (i + 1) * 16)
                if not (isinstance(i, int) and b < 2):
                    pe.wait_ge(xgT_copied, b - 1)
                nc.tensor.transpose(psXT[j % 2][:, 0:P], xg[j][:, 0:D], ident[:]).then_inc(xgT_ps_ready, 1)

            def layer1(i, j):
                b = i * R + j
                pe.wait_ge(xgT_copied, b + 1)
                pe.wait_ge(w_copied, b + 1)
                if not (isinstance(i, int) and b < 2):
                    pe.wait_ge(gelu_done, b - 1)
                for c in range(FC):
                    last = nc.tensor.matmul(psVG[:, j % 2, c * P:(c + 1) * P], wbuf[j % 3][:, c * P:(c + 1) * P], xgT[j % 2][:],
                                            start=True, stop=True)
                last.then_inc(h_ready, 1)

            def layer2(i, j, e):
                b = i * R + j
                pe.wait_ge(gelu_done, b + 1)
                if not (isinstance(i, int) and b < 2):
                    pe.wait_ge(dve_y, (b - 2) * Y_N + 1)
                for c in range(FC):
                    last = nc.tensor.matmul(psY[j % 2][:, 0:D], hid[j % 2][:, c, :],
                                            w2_sb[:, bass.ds(e, 1), c, :].rearrange("p a d -> p (a d)"),
                                            start=(c == 0), stop=(c == FC - 1))
                last.then_inc(y_ready, 1)

            pe.wait_ge(res_ready, SEQS)
            pe.wait_ge(dve_comb, SEQS * COMB_N)
            pe.wait_ge(gate_ready, SEQS)
            pe.wait_ge(w_loaded, (EXP + 2) * 16)
            transpose_rows(0, 0)

            def step(i, j):
                layer1(i, j)
                if not (isinstance(i, int) and i * R + j == 0):
                    e = pe.value_load(be[0:1, bass.ds(i * R + j - 1, 1)], min_val=0, max_val=EXP - 1)
                if not (isinstance(i, int) and i * R + j + 1 >= BLOCKS):
                    transpose_rows(*turn(i, j, 1, R))
                if not (isinstance(i, int) and i * R + j == 0):
                    layer2(*turn(i, j, -1, R), e)

            for j in range(R):
                step(0, j)
            with pe.Fori(1, BLOCKS // R - 1) as i:
                for j in range(R):
                    step(i, j)
            for j in range(R):
                step(BLOCKS // R - 1, j)
            layer2(BLOCKS // R - 1, R - 1, pe.value_load(be[0:1, BLOCKS - 1:BLOCKS], min_val=0, max_val=EXP - 1))

        @block.scalar
        def _(act):
            act.dma_start(wr_sb[:, 0:EXP], gate_w).then_inc(small_loaded, 16)
            act.dma_start(wr_sb[:, EXP:NL], Wgk).then_inc(small_loaded, 16)
            act.dma_start(bgk_bc[:], bgk.partition_broadcast(P)).then_inc(small_loaded, 16)
            for a in range(2):
                act.dma_start(gn_col[a * DV:(a + 1) * DV, :], gnorm_w.rearrange("(d a) -> d a", a=1)).then_inc(small_loaded, 16)
            act.dma_start(b1_rows[:], b1.rearrange("e (c f) -> (e c) f", f=P)).then_inc(small_loaded, 16)
            act.dma_start(wo_raw[:], Wo.rearrange("(a p) d -> p a d", p=P)).then_inc(proj_loaded, 16)
            act.dma_start(wq_sb[:], Wq).then_inc(proj_loaded, 16)
            act.dma_start(wk_sb[:], Wk).then_inc(proj_loaded, 16)
            act.dma_start(wvg_sb[:, 0:HV], Wv).then_inc(proj_loaded, 16)
            act.dma_start(wvg_sb[:, HV:2 * HV], Wg).then_inc(proj_loaded, 16)

            def copy_xt(i, q):
                g = i * 4 + q
                act.wait_ge(xt_ps_ready, g + 1)
                if not (isinstance(i, int) and g < 2):
                    s2, t2 = (q % 2, i * 2 + q // 2)
                    act.wait_ge(xt_stored[s2], t2 * 16)
                    act.wait_ge(lg_ready, g - 1)
                nc.scalar.copy(xts[q % 2][:], psA[:, q % 2, :]).then_inc(xts_ready, 1)

            def exp_step(i, q):
                g = i * 4 + q
                act.wait_ge(dve_max, (g + 1) * MAX_N)
                nc.scalar.activation(ex[q][:], d_all[:, bass.ds(g * GT, GT), :], ACT.Exp).then_inc(ex_ready, 1)

            def apply_norm(i, q):
                g = i * 4 + q
                act.wait_ge(nmr_ready, g + 1)
                if not (isinstance(i, int) and i == 0):
                    act.wait_ge(xw_stored[q], i * 16)
                for k in range(GT):
                    last = nc.scalar.activation(xw[q][:, k, 0:D], x_all[:, bass.ds(g * GT + k, 1), :].rearrange("p a d -> p (a d)"),
                                                ACT.Identity, bias=nmr[q][:, k:k + 1], scale=rstd[q][:, k:k + 1])
                last.then_inc(xn_ready, 1)

            def norm_step(i, q):
                if not (isinstance(i, int) and i * 4 + q < 3):
                    exp_step(*turn(i, q, -3, 4))
                if not (isinstance(i, int) and i * 4 + q < 1):
                    copy_xt(*turn(i, q, -1, 4))
                apply_norm(i, q)

            for q in range(4):
                norm_step(0, q)
            with act.Fori(1, GROUPS // 4) as i:
                for q in range(4):
                    norm_step(i, q)
            last = GROUPS // 4 - 1
            copy_xt(last, 3)
            exp_step(last, 1)
            exp_step(last, 2)
            exp_step(last, 3)

            act.wait_ge(dve_route, ROUTE["az"])
            nc.scalar.activation(ez[:], az[:], ACT.Exp, scale=-1.0).then_inc(act_route, 1)
            act.wait_ge(act_route, 1)
            nc.scalar.activation(l1[:], ez[:], ACT.Ln, bias=onesf[:, 0:1]).then_inc(act_route, 1)
            act.wait_ge(dve_route, ROUTE["gdiff"])
            nc.scalar.activation(e_k[:].rearrange("p t h -> p (t h)"), gdiff[:], ACT.Exp).then_inc(act_route, 1)
            nc.scalar.activation(e_q[:].rearrange("p t h -> p (t h)"), gc[:].rearrange("p t h -> p (t h)"), ACT.Exp).then_inc(act_route, 1)

            def copy_qk(i, j):
                s = i * 2 + j
                act.wait_ge(qk_ready, s + 1)
                if not (isinstance(i, int) and s == 0):
                    act.wait_ge(a_ready, s * 2)
                for h in range(H):
                    r = slice(h * DK, (h + 1) * DK)
                    nc.scalar.activation(qb[r, :, h, :], psQK[r, 0:SEQ].rearrange("p (k t) -> p k t", k=2), ACT.Copy, scale=float(DK) ** -0.5)
                if not (isinstance(i, int) and s < 2):
                    act.wait_ge(inter_ready, s - 1)
                nc.scalar.activation(qT1[j][:], psQK[:, P:SEQ], ACT.Copy, scale=float(DK) ** -0.5)
                nc.scalar.copy(kT[:], psQK[:, SEQ:2 * SEQ]).then_inc(qk_copied, 1)

            def tanh(i, j):
                s = i * 2 + j
                act.wait_ge(vg_ready, s + 1)
                if not (isinstance(i, int) and s == 0):
                    act.wait_ge(gate_ready, s)
                nc.scalar.activation(th[:], psVG[:, :, HV:2 * HV], ACT.Tanh, scale=0.5)

            def copy_v(i, j):
                s = i * 2 + j
                if not (isinstance(i, int) and s < 2):
                    act.wait_ge(o_ready, s - 1)
                nc.scalar.copy(v_sb[j][:], psVG[:, :, 0:HV]).then_inc(v_copied, 1)

            def exp_dec(i, j):
                s = i * 2 + j
                act.wait_ge(pool_dec, (s + 1) * 2)
                if not (isinstance(i, int) and s < 2):
                    act.wait_ge(p_ready, (s - 1) * 2)
                nc.scalar.activation(E[j][:].rearrange("p k n -> p (k n)"), gcB[j][:].rearrange("p h t -> p (h t)"), ACT.Exp).then_inc(e_ready, 1)

            def copy_o(i, j):
                s = i * 2 + j
                act.wait_ge(o_ready, s + 1)
                if not (isinstance(i, int) and s == 0):
                    act.wait_ge(dve_on, (s - 1) * ON_N + 1)
                nc.scalar.copy(oo[:].rearrange("p k n -> p (k n)"), psO[:]).then_inc(o_copied, 1)

            def copy_oT(i, j):
                s = i * 2 + j
                act.wait_ge(oT_ps_ready, s + 1)
                if not (isinstance(i, int) and s == 0):
                    act.wait_ge(wo_ready, s)
                nc.scalar.copy(oT[:].rearrange("p a t -> p (a t)"), psT[:]).then_inc(oT_copied, 1)

            act.wait_ge(pool_consts, POOL_CONSTS)
            copy_qk(0, 0)
            tanh(0, 0)
            copy_v(0, 0)
            exp_dec(0, 0)
            copy_qk(0, 1)
            tanh(0, 1)
            copy_v(0, 1)

            def step(i, j):
                copy_o(i, j)
                exp_dec(*turn(i, j, 1, 2))
                copy_qk(*turn(i, j, 2, 2))
                tanh(*turn(i, j, 2, 2))
                copy_v(*turn(i, j, 2, 2))
                copy_oT(i, j)

            step(0, 0)
            step(0, 1)
            with act.Fori(1, SEQS // 2 - 1) as i:
                for j in range(2):
                    step(i, j)
            last = SEQS // 2 - 1
            copy_o(last, 0)
            exp_dec(last, 1)
            copy_oT(last, 0)
            copy_o(last, 1)
            copy_oT(last, 1)

            psXT = [psQK, psKS]

            def copy_rows(i, j):
                b = i * R + j
                act.wait_ge(xgT_ps_ready, b + 1)
                if not (isinstance(i, int) and b < 2):
                    act.wait_ge(h_ready, b - 1)
                nc.scalar.copy(xgT[j % 2][:], psXT[j % 2][:, 0:P]).then_inc(xgT_copied, 1)

            def gelu(i, j):
                b = i * R + j
                act.wait_ge(h_ready, b + 1)
                if not (isinstance(i, int) and b < 2):
                    act.wait_ge(y_ready, b - 1)
                for c in range(FC):
                    last = nc.scalar.activation(hid[j % 2][:, c, :], psVG[:, j % 2, c * P:(c + 1) * P], ACT.Gelu,
                                                bias=wbuf[j % 3][:, FF + c:FF + c + 1])
                last.then_inc(gelu_done, 1)

            def step(i, j):
                if not (isinstance(i, int) and i * R + j + 1 >= BLOCKS):
                    copy_rows(*turn(i, j, 1, R))
                gelu(i, j)

            copy_rows(0, 0)
            for j in range(R):
                step(0, j)
            with act.Fori(1, BLOCKS // R - 1) as i:
                for j in range(R):
                    step(i, j)
            for j in range(R):
                step(BLOCKS // R - 1, j)

        @block.vector
        def _(dve):
            c_stats = Chain(dve, dve_stats, STATS_N)
            c_max = Chain(dve, dve_max, MAX_N)
            c_weight = Chain(dve, dve_weight, WEIGHT_N)

            def statistics(i, q):
                g = i * 4 + q
                c_stats.begin(g)
                dve.wait_ge(x_loaded[q], (i + 1) * 16)
                for k in range(GT):
                    c_stats.up(nc.vector.bn_stats(stats[q][:, k, :], x_all[:, bass.ds(g * GT + k, 1), :].rearrange("p a d -> p (a d)")))
                c_stats.wait()
                dve.sem_inc(tick, 1)
                for k in range(GT):
                    c_stats.up(nc.vector.bn_aggr(mv[q][:, k, :], stats[q][:, k, :]))
                c_stats.wait()
                c_stats.up(nc.vector.tensor_scalar(vpe[q][:], mv[q][:, :, 1], LN_EPS, None, ALU.add))
                c_stats.end()

            def mean_term(i, q):
                g = i * 4 + q
                if not (isinstance(i, int) and i == 0):
                    dve.wait_ge(xn_ready, g - 3)
                dve.wait_ge(rstd_ready, g + 1)
                nc.vector.scalar_tensor_tensor(nmr[q][:], mv[q][:, :, 0], -1.0, rstd[q][:], ALU.mult, ALU.mult).then_inc(nmr_ready, 1)

            def logit_max(i, q):
                g = i * 4 + q
                c_max.begin(g)
                dve.wait_ge(lg_ready, g + 1)
                rows = psVG[:, q % 2, 0:GT * NL].rearrange("p (k n) -> p k n", n=NL)
                c_max.up(nc.vector.tensor_reduce(lmax[q][:], rows[:, :, 0:EXP], AX.X, ALU.max))
                c_max.up(nc.vector.tensor_copy(lg_all[:, bass.ds(g * GT, GT), :], rows))
                c_max.wait()
                c_max.up(nc.vector.tensor_tensor(d_all[:, bass.ds(g * GT, GT), :], rows[:, :, 0:EXP],
                                                 lmax[q][:].unsqueeze(2).to_broadcast([P, GT, EXP]), ALU.subtract))
                c_max.end()

            def weight(i, q):
                g = i * 4 + q
                c_weight.begin(g)
                dve.wait_ge(ex_ready, g + 1)
                c_weight.up(nc.vector.tensor_reduce(sumex[q][:], ex[q][:], AX.X, ALU.add))
                c_weight.wait()
                c_weight.up(nc.vector.reciprocal(xw[q][:, :, D], sumex[q][:]))
                c_weight.end()

            dve.wait_ge(pool_consts, POOL_CONSTS)
            def norm_step(i, q):
                if not (isinstance(i, int) and i * 4 + q + 1 >= GROUPS):
                    statistics(*turn(i, q, 1, 4))
                mean_term(i, q)
                if not (isinstance(i, int) and i * 4 + q < 2):
                    logit_max(*turn(i, q, -2, 4))
                if not (isinstance(i, int) and i * 4 + q < 3):
                    weight(*turn(i, q, -3, 4))

            statistics(0, 0)
            for q in range(4):
                norm_step(0, q)
            with dve.Fori(1, GROUPS // 4 - 1) as i:
                for q in range(4):
                    norm_step(i, q)
            last = GROUPS // 4 - 1
            for q in range(4):
                norm_step(last, q)
            logit_max(last, 2)
            weight(last, 1)
            logit_max(last, 3)
            weight(last, 2)
            weight(last, 3)

            c = Chain(dve, dve_route, 0)
            c.begin(0)

            def then(ins, name=None):
                c.up(ins)
                if name:
                    assert ROUTE[name] == c.n, (name, c.n)
                c.wait()

            def bc(ap, shape):
                return ap.to_broadcast(shape)

            dve.wait_ge(dve_max, GROUPS * MAX_N)
            dve.wait_ge(small_loaded, SMALL * 16)
            then(nc.vector.tensor_tensor(z[:], lg_all[:, :, EXP:NL], bc(bgk_bc[:].unsqueeze(1), [P, TILES, H]), ALU.add))
            zf = z[:].rearrange("p t h -> p (t h)")
            then(nc.vector.scalar_tensor_tensor(az[:], zf, -1.0, zf, ALU.mult, ALU.max), "az")
            then(nc.vector.tensor_copy(rev[:], rev_i[:]))
            then(nc.vector.scalar_tensor_tensor(val[:], d_all[:], 0.0, bc(rev[:].unsqueeze(1), [P, TILES, EXP]), ALU.is_equal, ALU.mult))
            then(nc.vector.tensor_reduce(vmax[:], val[:], AX.X, ALU.max))
            then(nc.vector.tensor_tensor(onehot[:], val[:], bc(vmax[:].unsqueeze(2), [P, TILES, EXP]), ALU.is_equal), "onehot")
            dve.wait_ge(act_route, 2)
            then(nc.vector.scalar_tensor_tensor(g_all[:], zf, 0.0, l1[:], ALU.min, ALU.subtract))
            then(nc.vector.tensor_scalar(g_all[:], g_all[:], 1.0 / GATE_NORM, None, ALU.mult), "g")
            dve.wait_ge(pe_route, 1)
            gcf = gc[:].rearrange("p t h -> p (t h)")
            then(nc.vector.tensor_copy(gcf, psQK[:, 0:TH]), "gc")
            then(nc.vector.tensor_tensor(gdiff[:], psQK[:, TH:2 * TH], gcf, ALU.subtract), "gdiff")
            dve.wait_ge(pe_route, 3)
            then(nc.vector.tensor_copy(gcT[:].rearrange("p a t -> p (a t)"), psO[:, 0:2 * P]), "gcT")
            then(nc.vector.tensor_copy(w1b[:, :, FF:FF + FC], psO[:, 2 * P:2 * P + EXP * FC].rearrange("p (e c) -> p e c", c=FC)))
            dve.wait_ge(pe_route, 2)
            then(nc.vector.tensor_copy(pre[0][:, PAD:], psT[:, 0:TE]))
            k, a = EXP, 0
            while k < TE:
                then(nc.vector.tensor_tensor(pre[1 - a][:, PAD:], pre[a][:, PAD:], pre[a][:, PAD - k:PAD + TE - k], ALU.add))
                k, a = 2 * k, 1 - a
            total = pre[a][:, PAD + TE - EXP:]
            earlier = pre[a][:, PAD - EXP:PAD + TE - EXP].rearrange("p (t e) -> p t e", e=EXP)
            then(nc.vector.tensor_scalar(tot_i[:], total, float(P - 1), None, ALU.add))
            then(nc.vector.tensor_scalar(nb_i[:], tot_i[:], P.bit_length() - 1, None, ALU.arith_shift_right))
            then(nc.vector.tensor_copy(cb[0][:, EXP:], nb_i[:]))
            k, a = 1, 0
            while k < EXP:
                then(nc.vector.tensor_tensor(cb[1 - a][:, EXP:], cb[a][:, EXP:], cb[a][:, EXP - k:2 * EXP - k], ALU.add))
                k, a = 2 * k, 1 - a
            upto_e = cb[a][:, EXP:]
            then(nc.vector.tensor_scalar(base[:], cb[a][:, EXP - 1:2 * EXP - 1], float(P), None, ALU.mult))
            then(nc.vector.tensor_tensor(slot_f[:], psKS[:, 0:TE].rearrange("p (t e) -> p t e", e=EXP), earlier, ALU.add))
            then(nc.vector.tensor_tensor(slot_f[:], slot_f[:], bc(base[:].unsqueeze(1), [P, TILES, EXP]), ALU.add))
            then(nc.vector.tensor_tensor(slot_f[:], slot_f[:], onehot[:], ALU.mult))
            then(nc.vector.tensor_reduce(pos[:], slot_f[:], AX.X, ALU.add))
            then(nc.vector.tensor_copy(pos_i[:], pos[:]))
            then(nc.vector.tensor_scalar(lo_i[:], pos_i[:], P - 1, None, ALU.bitwise_and))
            then(nc.vector.tensor_scalar(hi_i[:], pos_i[:], P.bit_length() - 1, None, ALU.arith_shift_right))
            then(nc.vector.scalar_tensor_tensor(place[:, :, 0], lo_i[:], BLOCKS, hi_i[:], ALU.mult, ALU.add))
            then(nc.vector.tensor_copy(place[:, :, 1], ids[:]))
            then(nc.vector.tensor_copy(iota_f[:], iota_i[:]))
            dve.wait_ge(proj_loaded, 16 * 5)
            for a in range(2):
                then(nc.vector.tensor_scalar(wo_sb[:, a, :], wo_raw[:, a, :], gn_col[:, 0:1], 0.5, ALU.mult, ALU.mult))
            then(nc.vector.tensor_tensor(isge[:], bc(iota_f[:, 0:BLOCKS].unsqueeze(2), [P, BLOCKS, EXP - 1]),
                                         bc(upto_e[:, 0:EXP - 1].unsqueeze(1), [P, BLOCKS, EXP - 1]), ALU.is_ge))
            then(nc.vector.tensor_reduce(be_f[:], isge[:], AX.X, ALU.add))
            then(nc.vector.tensor_copy(be[:], be_f[:]), "all")
            dve.wait_ge(act_route, 4)

            def finish_table():
                dve.wait_ge(table_loaded, 16)
                nc.vector.tensor_scalar(gid[:], sid[:], TOKENS - 1, None, ALU.min).then_inc(gid_ready, 1)
                dve.wait_ge(gid_ready, 1)

            def copy_place(i, j):
                s = i * 2 + j
                if not (isinstance(i, int) and s < 2):
                    dve.wait_ge(placed[j], i * 32)
                nc.vector.tensor_copy(place_s[j][:], place[:, bass.ds(s * 2, 2), :]).then_inc(place_ready, 1)

            c_comb = Chain(dve, dve_comb, COMB_N)
            c_on = Chain(dve, dve_on, ON_N)

            def combine(i, j):
                s = i * 2 + j
                c_comb.begin(s)
                dve.wait_ge(inter_ready, s + 1)
                c_comb.up(nc.vector.tensor_tensor(inter[:].rearrange("p (h d) -> p h d", d=DV), psKS[:, 0:HV].rearrange("p (h d) -> p h d", d=DV),
                                                  bc(e_q[:, bass.ds(s * 2 + 1, 1), :].rearrange("p a h -> p (a h)").unsqueeze(2), [P, H, DV]), ALU.mult))
                c_comb.wait()
                dve.wait_ge(o_copied, s + 1)
                c_comb.up(nc.vector.tensor_tensor(oo[:, 1, :], inter[:], oo[:, 1, :], ALU.add))
                c_comb.wait()
                c_comb.up(nc.vector.tensor_tensor(sq[:], oo[:], oo[:], ALU.mult))
                c_comb.wait()
                c_comb.up(nc.vector.tensor_reduce(ms[:], sq[:].rearrange("p k (h d) -> p (k h) d", d=DV), AX.X, ALU.add))
                c_comb.wait()
                c_comb.up(nc.vector.tensor_scalar(msn[:], ms[:], 1.0 / DV, RMS_EPS, ALU.mult, ALU.add))
                c_comb.end()

            def probs(i, j):
                s = i * 2 + j
                dve.wait_ge(e_ready, s + 1)
                if not (isinstance(i, int) and s == 0):
                    dve.wait_ge(o_ready, s)
                for k in range(2):
                    dve.wait_ge(a_ready, s * 2 + k + 1)
                    nc.vector.tensor_tensor(pr[:, k, :], psA[:, k, :], E[j][:, k, :], ALU.mult).then_inc(p_ready, 1)

            def decay_k(i, j):
                s = i * 2 + j
                dve.wait_ge(k0_ready, s + 1)
                nc.vector.tensor_tensor(kd[:].rearrange("p (h d) -> p h d", d=DK), psKS[:, 0:P].rearrange("p (h d) -> p h d", d=DK),
                                        bc(e_k[:, bass.ds(s * 2, 1), :].rearrange("p a h -> p (a h)").unsqueeze(2), [P, H, DK]), ALU.mult).then_inc(kd_ready, 1)

            def normed(i, j):
                s = i * 2 + j
                c_on.begin(s)
                c_on.up(nc.vector.tensor_tensor(og[:], oo[:], gate[j][:], ALU.mult))
                c_on.wait()
                dve.wait_ge(rms_ready, s + 1)
                if not (isinstance(i, int) and s == 0):
                    dve.wait_ge(oT_ps_ready, s)
                c_on.up(nc.vector.tensor_tensor(on[:].rearrange("p k (h d) -> p (k h) d", d=DV), og[:].rearrange("p k (h d) -> p (k h) d", d=DV),
                                                bc(rms[:].unsqueeze(2), [P, 2 * H, DV]), ALU.mult))
                c_on.end()

            def copy_state(i, j):
                s = i * 2 + j
                dve.wait_ge(s_ready, s + 1)
                if not (isinstance(i, int) and s == 0):
                    dve.wait_ge(inter_ready, s)
                nc.vector.tensor_tensor(S_sb[:], psKS[:, HV:2 * HV], headmask[:], ALU.mult).then_inc(s_copied, 1)

            def make_gate(i, j):
                s = i * 2 + j
                dve.wait_ge(v_copied, s + 1)
                nc.vector.scalar_tensor_tensor(gate[j][:], th[:], 1.0, psVG[:, :, HV:2 * HV], ALU.add, ALU.mult).then_inc(gate_ready, 1)

            def residual(i, j):
                s = i * 2 + j
                dve.wait_ge(wo_ready, s + 1)
                if not (isinstance(i, int) and s < 2):
                    dve.wait_ge(res_stored[j], i * 16)
                nc.vector.tensor_tensor(res[j][:], psT[:, 0:2 * D].rearrange("p (k d) -> p k d", d=D), x_all[:, bass.ds(s * 2, 2), :],
                                        ALU.add).then_inc(res_ready, 1)

            for j in range(2):
                copy_place(0, j)
            def copy_gidx(i, j):
                b = i * R + j
                if not (isinstance(i, int) and i == 0):
                    dve.wait_ge(gathered[j], i * 16)
                nc.vector.tensor_copy(gidx[j][:], gid[:, bass.ds(b, 1)]).then_inc(gidx_ready, 1)

            make_gate(0, 0)
            probs(0, 0)
            decay_k(0, 0)
            copy_state(0, 0)
            make_gate(0, 1)
            combine(0, 0)
            probs(0, 1)
            decay_k(0, 1)
            normed(0, 0)
            copy_state(0, 1)
            make_gate(1, 0)
            copy_place(1, 0)

            def step(i, j):
                combine(*turn(i, j, -1, 2))
                probs(i, j)
                decay_k(i, j)
                normed(*turn(i, j, -1, 2))
                copy_state(i, j)
                make_gate(*turn(i, j, 1, 2))
                residual(i - 1, j)
                copy_place(*turn(i, j, 1, 2))

            with dve.Fori(1, SEQS // 2 - 1) as i:
                for j in range(2):
                    step(i, j)
            last = SEQS // 2 - 1
            combine(last - 1, 1)
            probs(last, 0)
            decay_k(last, 0)
            normed(last - 1, 1)
            copy_state(last, 0)
            make_gate(last, 1)
            residual(last - 1, 0)
            copy_place(last, 1)
            combine(last, 0)
            probs(last, 1)
            decay_k(last, 1)
            normed(last, 0)
            copy_state(last, 1)
            residual(last - 1, 1)
            combine(last, 1)
            normed(last, 1)
            finish_table()
            for j in range(R):
                copy_gidx(0, j)
            residual(last, 0)
            residual(last, 1)

            c_y = Chain(dve, dve_y, Y_N)
            psY = [psO, psT]

            def copy_w(i, j):
                b = i * R + j
                e = dve.value_load(be[0:1, bass.ds(b, 1)], min_val=0, max_val=EXP - 1)
                if not (isinstance(i, int) and b < 2):
                    dve.wait_ge(gelu_done, b - 1)
                nc.vector.tensor_copy(wbuf[j % 3], w1b[:, bass.ds(e, 1), :].rearrange("p a n -> p (a n)")).then_inc(w_copied, 1)

            def weigh(i, j):
                b = i * R + j
                c_y.begin(b)
                if not (isinstance(i, int) and i == 0):
                    dve.wait_ge(scattered[j], i * 16)
                nc.vector.tensor_copy(sidx[j][:], sid[:, bass.ds(b, 1)]).then_inc(sidx_ready, 1)
                dve.wait_ge(y_ready, b + 1)
                c_y.up(nc.vector.tensor_tensor(yb[j % 2][:], psY[j % 2][:, 0:D], wbuf[j % 3][:, FF + FC:WB], ALU.add))
                c_y.wait()
                dve.wait_ge(gathered[j], (i + 1) * 16)
                c_y.up(nc.vector.tensor_scalar(yw[j][:], yb[j % 2][:], xg[j][:, D:D + 1], None, ALU.mult))
                c_y.end()

            dve.wait_ge(w_loaded, (EXP + 2) * 16)
            copy_w(0, 0)
            copy_w(0, 1)

            def step(i, j):
                if not (isinstance(i, int) and i * R + j + 2 >= BLOCKS):
                    copy_w(*turn(i, j, 2, R))
                if not (isinstance(i, int) and i + 1 >= BLOCKS // R):
                    copy_gidx(i + 1, j)
                weigh(i, j)

            for j in range(R):
                step(0, j)
            with dve.Fori(1, BLOCKS // R - 1) as i:
                for j in range(R):
                    step(i, j)
            for j in range(R):
                step(BLOCKS // R - 1, j)


POOL_CONSTS = 22
SMALL = 6
ROUTE = {"az": 2, "onehot": 6, "g": 8, "gc": 9, "gdiff": 10, "gcT": 11, "all": 41}


_INS = ["L0_attn_x", "L0_attn_Wq", "L0_attn_Wk", "L0_attn_Wv", "L0_attn_Wg", "L0_attn_Wgk", "L0_attn_bgk", "L0_attn_Wo",
        "L0_attn_gnorm_w", "L0_ffn_gate_w", "L0_ffn_w1", "L0_ffn_b1", "L0_ffn_w2", "L0_ffn_b2"]


def kernel(**inputs):
    import numpy as _np
    import concourse.bacc as _bacc
    from concourse import mybir as _mybir
    from concourse.bass_utils import run_bass_kernel_spmd as _run

    nc = _bacc.Bacc("TRN2", target_bir_lowering=False, num_devices=1)
    arrays, args = {}, []
    for name in _INS:
        a = _np.ascontiguousarray(inputs[name])
        arrays[f"in_{name}_dram"] = a
        args.append(nc.dram_tensor(f"in_{name}_dram", a.shape, _mybir.dt.from_np(a.dtype), kind="ExternalInput").ap())
    shape = inputs["L0_attn_x"].shape
    args.append(nc.dram_tensor("out_0_dram", shape, _mybir.dt.float32, kind="ExternalOutput").ap())
    build_layer(nc, *args)
    r = _run(nc, [arrays], core_ids=[0])
    return r.results[0]["out_0_dram"]
```

```python
from contextlib import ExitStack

import concourse.bass as bass
from concourse import mybir

ALU = mybir.AluOpType
ACT = mybir.ActivationFunctionType
AX = mybir.AxisListType
F32 = mybir.dt.float32
BF16 = mybir.dt.bfloat16
I32 = mybir.dt.int32
F32R = mybir.dt.float32r

P = 128
LN_EPS = 1e-5
RMS_EPS = 1e-5
GATE_NORM = 16.0
MASKED = -1e30


def turn(i, j, d, n):
    return i + (j + d) // n, (j + d) % n


class Chain:

    def __init__(self, eng, sem, per_step):
        self.eng, self.sem, self.per_step = eng, sem, per_step

    def begin(self, step):
        self.base, self.n = step * self.per_step, 0

    def up(self, ins):
        ins.then_inc(self.sem, 1)
        self.n += 1

    def wait(self):
        self.eng.wait_ge(self.sem, self.base + self.n)

    def end(self):
        assert self.n == self.per_step


def build_layer(nc, x, Wq, Wk, Wv, Wg, Wgk, bgk, Wo, gnorm_w, gate_w, w1, b1, w2, b2, out):
    SEQS, SEQ, D = x.shape
    TOKENS = SEQS * SEQ
    TILES = TOKENS // P
    H = Wgk.shape[1]
    DK = Wq.shape[1] // H
    DV = Wv.shape[1] // H
    HV = H * DV
    EXP, _, FF = w1.shape
    FC = FF // P
    NL = EXP + H
    assert D == P and H * DK == P and SEQ == 2 * P and HV == 2 * P and FF == 4 * P

    GT = 4
    GROUPS = TILES // GT
    R = 8
    BLOCKS = TILES + EXP - 1
    TURNS = -(-BLOCKS // R)
    TAIL = BLOCKS - (TURNS - 1) * R
    ROWS = TURNS * R
    XW = D + 2
    BR = ROWS // (GROUPS - 4)
    WB = FF + FC + D
    TE = TILES * EXP
    TH = TILES * H
    KC = TE // P
    BAND = (2 * KC - 1) * P

    x_t = x.rearrange("s (k p) d -> p (s k) d", p=P)
    out_rows = out.rearrange("s n d -> (s n) d")
    out_t = out.rearrange("s (k p) d -> p (s k) d", p=P)
    sorted_dram = nc.dram_tensor("sorted_rows", [ROWS * P, XW], F32).ap()
    xt_dram = nc.dram_tensor("xn_transposed", [GROUPS, P, GT * P], F32).ap()
    gc_dram = nc.dram_tensor("decay_rows", [TH, P], F32).ap()

    with ExitStack() as ctx:
        def sb(name, shape, dt=F32):
            return ctx.enter_context(nc.sbuf_tensor(name, shape, dt))

        def ps(name, shape):
            return ctx.enter_context(nc.psum_tensor(name, shape, F32))

        def sem(name):
            return ctx.enter_context(nc.semaphore(name))

        ident = sb("ident", [P, P])
        upto = sb("upto", [P, P])
        onesf = sb("onesf", [P, P])
        before = sb("before", [P, P], BF16)
        onesb = sb("onesb", [P, P], BF16)
        band_i = sb("band_i", [P, BAND], I32)
        band = sb("band", [P, BAND], BF16)
        iota_i = sb("iota_i", [P, P], I32)
        iota_f = sb("iota_f", [P, P])
        ids = sb("ids", [P, TILES], I32)
        rev_i = sb("rev_i", [P, EXP], I32)
        rev = sb("rev", [P, EXP])
        warm = sb("warm", [P, 8])
        neg_half = sb("neg_half", [P, 8])
        headmask = sb("headmask", [P, HV])
        wq_sb = sb("wq_sb", [P, H * DK])
        wk_sb = sb("wk_sb", [P, H * DK])
        wvg_sb = sb("wvg_sb", [P, 2 * HV])
        w_hi = sb("w_hi", [P, 2 * H * DK + 2 * HV], F32R)
        w_lo = sb("w_lo", [P, 2 * H * DK + 2 * HV], F32R)
        wr_sb = sb("wr_sb", [P, NL])
        wo_raw = sb("wo_raw", [P, 2, D])
        wo_sb = sb("wo_sb", [P, 2, D])
        gn_col = sb("gn_col", [P, 1])
        bgk_bc = sb("bgk_bc", [P, H])
        b1_rows = sb("b1_rows", [EXP * FC, P])
        w1b = sb("w1b", [P, EXP, WB])
        w2_sb = sb("w2_sb", [P, EXP, FC, D])

        x_all = sb("x_all", [P, TILES, D])
        stats = [sb(f"stats{q}", [P, GT, 6]) for q in range(4)]
        mv = [sb(f"mv{q}", [P, GT, 2]) for q in range(4)]
        vpe = [sb(f"vpe{q}", [P, GT]) for q in range(4)]
        rstd = sb("rstd", [P, TILES])
        nmr = sb("nmr", [P, TILES])
        xn = [sb(f"xn{q}", [P, GT, D]) for q in range(4)]
        xts = [sb(f"xts{q}", [P, GT * P]) for q in range(2)]
        lmax = sb("lmax", [P, TILES])
        d_all = sb("d_all", [P, TILES, EXP])
        ex = sb("ex", [P, TILES, EXP])
        sumex = sb("sumex", [P, TILES])

        z = sb("z", [P, TILES, H])
        az = sb("az", [P, TH])
        ez = sb("ez", [P, TH])
        l1 = sb("l1", [P, TH])
        g_all = sb("g_all", [P, TH])
        gc = sb("gc", [P, TILES, H])
        gdiff = sb("gdiff", [P, TH])
        e_k = sb("e_k", [P, TILES, H])
        e_q = sb("e_q", [P, TILES, H])
        gcT = sb("gcT", [P, 2, P])
        val = sb("val", [P, TILES, EXP])
        vmax = sb("vmax", [P, TILES])
        onehot = sb("onehot", [P, TILES, EXP], BF16)
        count = sb("count", [P, KC], BF16)
        count_bc = sb("count_bc", [P, KC, P], BF16)
        tot_i = sb("tot_i", [P, EXP], I32)
        nb_i = sb("nb_i", [P, EXP], I32)
        cb = [sb(f"cb{q}", [P, 2 * EXP]) for q in range(2)]
        base = sb("base", [P, EXP])
        slot_f = sb("slot_f", [P, TILES, EXP])
        pos = sb("pos", [P, TILES])
        pos_i = sb("pos_i", [P, TILES], I32)
        extra = sb("extra", [P, TILES, 2])
        rows = [sb(f"rows{j}", [P, 2, XW]) for j in range(2)]
        pos_s = [sb(f"pos{j}", [P, 2], I32) for j in range(2)]
        blank = sb("blank", [P, BR, XW])
        isge = sb("isge", [P, BLOCKS, EXP - 1])
        be_f = sb("be_f", [P, BLOCKS])
        be = sb("be", [P, BLOCKS], I32)

        xT = [sb(f"xT{j}", [P, SEQ]) for j in range(2)]
        x_hi = [sb(f"x_hi{j}", [P, SEQ], F32R) for j in range(2)]
        x_lo = [sb(f"x_lo{j}", [P, SEQ], F32R) for j in range(2)]
        gcB = [sb(f"gcB{j}", [P, 2 * H, P]) for j in range(2)]
        E = [sb(f"E{j}", [P, 2, H * P]) for j in range(2)]
        qb = sb("qb", [P, 2, H, P])
        qT1 = [sb(f"qT1{j}", [P, P]) for j in range(2)]
        kT = sb("kT", [P, SEQ])
        v_sb = [sb(f"v_sb{j}", [P, 2, HV]) for j in range(2)]
        th = sb("th", [P, 2, HV])
        gate = [sb(f"gate{j}", [P, 2, HV]) for j in range(2)]
        kd = sb("kd", [P, H * DK])
        S_sb = sb("S_sb", [P, HV])
        pr = sb("pr", [P, 2, H * P])
        inter = sb("inter", [P, HV])
        oo = sb("oo", [P, 2, HV])
        sq = sb("sq", [P, 2, HV])
        ms = sb("ms", [P, 2 * H])
        msn = sb("msn", [P, 2 * H])
        rms = sb("rms", [P, 2 * H])
        og = sb("og", [P, 2, HV])
        on = sb("on", [P, 2, HV])
        oT = sb("oT", [P, 4, P])
        res = [sb(f"res{j}", [P, 2, D]) for j in range(2)]

        sidx = [sb(f"sidx{j}", [P, 1], I32) for j in range(R)]
        xg = [sb(f"xg{j}", [P, XW]) for j in range(R)]
        xgT = [sb(f"xgT{j}", [P, P]) for j in range(2)]
        wbuf = [t[:].rearrange("p k n -> p (k n)")[:, 0:WB] for t in (E[0], E[1], gcB[0], gcB[1])]
        hid = [t[:].rearrange("p k (c n) -> p (k c) n", n=P) for t in (sq, og)]
        yb = [sb(f"yb{j}", [P, D]) for j in range(2)]
        yw = [sb(f"yw{j}", [P, D]) for j in range(R)]

        psQK = ps("psQK", [P, 512])
        psVG = ps("psVG", [P, 2, 512])
        psKS = ps("psKS", [P, 512])
        psA = ps("psA", [P, 2, 512])
        psO = ps("psO", [P, 512])
        psT = ps("psT", [P, 512])

        ps_logits = psVG[:].rearrange("p a (t n) -> p (a t) n", n=2 * 512 // TILES)

        x_loaded = [sem(f"x_loaded{q}") for q in range(4)]
        wr_loaded = sem("wr_loaded")
        small_loaded = sem("small_loaded")
        proj_loaded = sem("proj_loaded")
        w_loaded = sem("w_loaded")
        xt_stored = [sem(f"xt_stored{q}") for q in range(2)]
        gc_stored = [sem(f"gc_stored{a}") for a in range(2)]
        xT_loaded = [sem(f"xT_loaded{j}") for j in range(2)]
        gcB_loaded = [sem(f"gcB_loaded{j}") for j in range(2)]
        res_stored = [sem(f"res_stored{j}") for j in range(2)]
        xg_loaded = [sem(f"xg_loaded{j}") for j in range(R)]
        scattered = [sem(f"scattered{j}") for j in range(R)]
        pool_consts = sem("pool_consts")
        dve_stats = sem("dve_stats")
        rstd_ready = sem("rstd_ready")
        nmr_ready = sem("nmr_ready")
        xn_ready = sem("xn_ready")
        xt_ps_ready = sem("xt_ps_ready")
        xts_ready = sem("xts_ready")
        lg_ready = sem("lg_ready")
        dve_route = sem("dve_route")
        act_route = sem("act_route")
        pe_route = sem("pe_route")
        blank_made = sem("blank_made")
        first_consts = sem("first_consts")
        band_step = sem("band_step")
        first_band = sem("first_band")
        dve_late = sem("dve_late")
        wo_scaled = sem("wo_scaled")
        sort_cleared = sem("sort_cleared")
        xn_rows_ready = sem("xn_rows_ready")
        rows_ready = sem("rows_ready")
        placed = [sem(f"placed{j}") for j in range(2)]
        w_split = sem("w_split")
        hi_ready = sem("hi_ready")
        lo_ready = sem("lo_ready")
        qk_ready = sem("qk_ready")
        vg_ready = sem("vg_ready")
        a_ready = sem("a_ready")
        k0_ready = sem("k0_ready")
        s_ready = sem("s_ready")
        o_ready = sem("o_ready")
        inter_ready = sem("inter_ready")
        oT_ps_ready = sem("oT_ps_ready")
        wo_ready = sem("wo_ready")
        qk_copied = sem("qk_copied")
        v_copied = sem("v_copied")
        o_copied = sem("o_copied")
        e_ready = sem("e_ready")
        oT_copied = sem("oT_copied")
        dve_comb = sem("dve_comb")
        p_ready = sem("p_ready")
        kd_ready = sem("kd_ready")
        dve_on = sem("dve_on")
        s_copied = sem("s_copied")
        gate_ready = sem("gate_ready")
        res_ready = sem("res_ready")
        pool_dec = sem("pool_dec")
        rms_ready = sem("rms_ready")
        tick = sem("tick")
        sidx_ready = sem("sidx_ready")
        xgT_ps_ready = sem("xgT_ps_ready")
        xgT_copied = sem("xgT_copied")
        w_copied = sem("w_copied")
        h_ready = sem("h_ready")
        gelu_done = sem("gelu_done")
        y_ready = sem("y_ready")
        dve_y = sem("dve_y")

        STATS_N = 9
        W_LOADS = 1 + EXP * (1 + FC)
        COMB_N, ON_N, Y_N = 5, 2, 2
        LAST = SEQS - 1

        block = ctx.enter_context(nc.Block())

        @block.sync
        def _(sp):
            def load_x(i, q):
                if not (isinstance(i, int) and i == 0):
                    sp.wait_ge(x_loaded[q], i * 16)
                g = i * 4 + q
                sp.dma_start(x_all[:, bass.ds(g * GT, GT), :], x_t[:, bass.ds(g * GT, GT), :]).then_inc(x_loaded[q], 16)

            def store_xt(i, q):
                g = i * 4 + q
                sp.wait_ge(xts_ready, g + 1)
                sp.dma_start(xt_dram[bass.ds(g, 1), :, :].rearrange("a p n -> p (a n)"), xts[q % 2][:]).then_inc(xt_stored[q % 2], 16)

            def norm_step(i, q):
                if not (isinstance(i, int) and i + 2 >= GROUPS // 4):
                    load_x(i + 2, q)
                if not (isinstance(i, int) and i * 4 + q < 1):
                    store_xt(*turn(i, q, -1, 4))

            for i in range(2):
                for q in range(4):
                    load_x(i, q)
            for q in range(4):
                norm_step(0, q)
            sp.dma_start(bgk_bc[:], bgk.partition_broadcast(P)).then_inc(small_loaded, 16)
            for a in range(2):
                sp.dma_start(gn_col[a * DV:(a + 1) * DV, :], gnorm_w.rearrange("(d a) -> d a", a=1)).then_inc(small_loaded, 16)
            sp.dma_start(b1_rows[:], b1.rearrange("e (c f) -> (e c) f", f=P)).then_inc(small_loaded, 16)
            sp.dma_start(wo_raw[:], Wo.rearrange("(a p) d -> p a d", p=P)).then_inc(proj_loaded, 16)
            sp.dma_start(wq_sb[:], Wq).then_inc(proj_loaded, 16)
            sp.dma_start(wk_sb[:], Wk).then_inc(proj_loaded, 16)
            sp.dma_start(wvg_sb[:, 0:HV], Wv).then_inc(proj_loaded, 16)
            sp.dma_start(wvg_sb[:, HV:2 * HV], Wg).then_inc(proj_loaded, 16)
            cleared = sorted_dram.rearrange("(p a n) c -> p a n c", p=P, n=BR)

            def clear(i, q):
                sp.dma_start(cleared[:, bass.ds((i - 1) * 4 + q, 1), :, :].rearrange("p a n c -> p (a n) c"), blank[:]).then_inc(sort_cleared, 16)

            sp.wait_ge(blank_made, 2)
            with sp.Fori(1, GROUPS // 4 - 2) as i:
                for q in range(4):
                    norm_step(i, q)
                    clear(i, q)

            def load_xt(i, j):
                sp.dma_start(xT[j][:], xt_dram[bass.ds(i, 1), :, j * SEQ:(j + 1) * SEQ].rearrange("a p n -> p (a n)")).then_inc(xT_loaded[j], 16)

            sp.wait_ge(xt_stored[0], 16)
            for j in range(2):
                load_xt(0, j)
            for i in range(GROUPS // 4 - 2, GROUPS // 4):
                for q in range(4):
                    norm_step(i, q)
                    clear(i, q)
            store_xt(GROUPS // 4 - 1, 3)

            for q in range(2):
                sp.wait_ge(xt_stored[q], GROUPS // 2 * 16)
            gc_rows = gc_dram.rearrange("(a p) t -> p a t", p=P)
            sp.wait_ge(act_route, 3)
            for a in range(2):
                sp.dma_start(gc_rows[:, a, :], gcT[:, a, :]).then_inc(gc_stored[a], 16)

            sp.wait_ge(gc_stored[0], 16)

            def load_gc(i, j):
                s = i * 2 + j
                sp.dma_start(gcB[j][:].rearrange("p h t -> p (h t)"),
                             gc_dram[bass.ds(s * 2 * H, 2 * H), :].rearrange("r t -> (r t)").partition_broadcast(P)).then_inc(gcB_loaded[j], 16)

            def store_res(i, j):
                s = i * 2 + j
                sp.wait_ge(res_ready, s + 1)
                sp.dma_start(out_t[:, bass.ds(s * 2, 2), :], res[j][:]).then_inc(res_stored[j], 16)

            for j in range(2):
                load_gc(0, j)

            def step(i, j):
                s = i * 2 + j
                sp.wait_ge(lo_ready, s + 1)
                load_xt(i + 1, j)
                sp.wait_ge(e_ready, s + 1)
                load_gc(i + 1, j)

            for j in range(2):
                step(0, j)
            sp.wait_ge(gc_stored[1], 16)
            sp.dma_start(w1b[:, :, FF + FC:WB], b2.partition_broadcast(P)).then_inc(w_loaded, 16)
            with sp.Fori(1, 1 + EXP // 2) as i:
                for j in range(2):
                    step(i, j)
                    store_res(i - 1, j)
                    e = bass.ds((i - 1) * 2 + j, 1)
                    sp.dma_start(w1b[:, e, 0:FF], w1[e, :, :].rearrange("e d f -> d e f")).then_inc(w_loaded, 16)
                    for c in range(FC):
                        sp.dma_start(w2_sb[:, e, c, :], w2[e, c * P:(c + 1) * P, :].rearrange("e f d -> f e d")).then_inc(w_loaded, 16)
            with sp.Fori(1 + EXP // 2, SEQS // 2 - 1) as i:
                for j in range(2):
                    step(i, j)
                    store_res(i - 1, j)
            for j in range(2):
                store_res(SEQS // 2 - 2, j)

            def load_block(i, j):
                b = i * R + j
                if not (isinstance(i, int) and i == 0):
                    sp.wait_ge(dve_y, (b - R + 1) * Y_N)
                sp.dma_start(xg[j][:], sorted_dram[bass.ds(b * P, P), :]).then_inc(xg_loaded[j], 16)

            for j in range(2):
                sp.wait_ge(placed[j], SEQS // 2 * 32)
            for j in range(R):
                load_block(0, j)
            for j in range(2):
                store_res(SEQS // 2 - 1, j)
            with sp.Fori(1, TURNS - 1) as i:
                for j in range(R):
                    load_block(i, j)
            for j in range(TAIL):
                load_block(TURNS - 1, j)
            for j in range(2):
                sp.wait_ge(res_stored[j], SEQS // 2 * 16)

        @block.gpsimd
        def _(pool):
            c = [0]

            def const(ins):
                ins.then_inc(pool_consts, 1)
                c[0] += 1

            nc.gpsimd.memset(neg_half[:], -0.5).then_inc(first_consts, 1)
            nc.gpsimd.memset(ident[:], 1.0).then_inc(first_consts, 1)
            pool.wait_ge(first_consts, 2)
            nc.gpsimd.affine_select(out=ident[:], in_=ident[:], pattern=[[1, P]], compare_op=ALU.is_equal,
                                    fill=0.0, base=0, channel_multiplier=-1).then_inc(first_consts, 1)
            const(nc.gpsimd.iota(band_i[:], pattern=[[1, BAND]], base=-(KC - 1) * P + BAND, channel_multiplier=-1))
            const(nc.gpsimd.memset(upto[:], 1.0))
            const(nc.gpsimd.memset(onesf[:], 1.0))
            const(nc.gpsimd.memset(before[:], 1.0))
            const(nc.gpsimd.memset(onesb[:], 1.0))

            def rstd_step(i, q):
                g = i * 4 + q
                pool.wait_ge(dve_stats, (g + 1) * STATS_N)
                nc.gpsimd.tensor_tensor(rstd[:, bass.ds(g * GT, GT)], vpe[q][:], neg_half[:, 0:GT], ALU.pow).then_inc(rstd_ready, 1)

            rstd_step(0, 0)
            pool.wait_ge(pool_consts, c[0])
            const(nc.gpsimd.affine_select(out=upto[:], in_=upto[:], pattern=[[1, P]], compare_op=ALU.is_ge,
                                          fill=0.0, base=0, channel_multiplier=-1))
            const(nc.gpsimd.affine_select(out=before[:], in_=before[:], pattern=[[1, P]], compare_op=ALU.is_ge,
                                          fill=0.0, base=-1, channel_multiplier=-1))
            rstd_step(0, 1)
            const(nc.gpsimd.memset(headmask[:], 0.0))
            for q in range(2):
                const(nc.gpsimd.memset(cb[q][:, 0:EXP], 0.0))
            const(nc.gpsimd.iota(iota_i[:], pattern=[[1, P]], base=0, channel_multiplier=0))
            const(nc.gpsimd.iota(ids[:], pattern=[[P, TILES]], base=0, channel_multiplier=1))
            const(nc.gpsimd.iota(rev_i[:], pattern=[[-1, EXP]], base=EXP, channel_multiplier=0))
            rstd_step(0, 2)
            for h in range(H):
                pool.wait_ge(pool_consts, c[0])
                const(nc.gpsimd.memset(headmask[h * DK:(h + 1) * DK, h * DV:(h + 1) * DV], 1.0))
            pool.wait_ge(pool_consts, c[0])
            rstd_step(0, 3)
            const(nc.gpsimd.memset(qb[:], 0.0))
            nc.gpsimd.memset(blank[:], 0.0).then_inc(blank_made, 1)
            pool.wait_ge(blank_made, 1)
            nc.gpsimd.memset(blank[:, :, D + 1:D + 2], float(TOKENS)).then_inc(blank_made, 1)
            pool.wait_ge(first_band, 1)
            const(nc.gpsimd.affine_select(out=band[:], in_=band[:], pattern=[[1, BAND]], compare_op=ALU.is_ge,
                                          fill=0.0, base=-(KC - 1) * P - 1, channel_multiplier=-1))
            assert c[0] == POOL_CONSTS
            with pool.Fori(1, GROUPS // 4) as i:
                for q in range(4):
                    rstd_step(i, q)

            def dec(i, j):
                s = i * 2 + j
                pool.wait_ge(gcB_loaded[j], (i + 1) * 16)
                nc.gpsimd.tensor_tensor(gcB[j][:], gcB[j][:],
                                        gc[:, bass.ds(s * 2, 2), :].rearrange("p k h -> p (k h)").unsqueeze(2).to_broadcast([P, 2 * H, P]),
                                        ALU.subtract).then_inc(pool_dec, 1)
                pool.wait_ge(pool_dec, s * 2 + 1)
                pool.sem_inc(tick, 1)
                nc.gpsimd.affine_select(out=gcB[j][:], in_=gcB[j][:], pattern=[[0, 2 * H], [1, P]], compare_op=ALU.is_ge,
                                        fill=MASKED, base=0, channel_multiplier=-1).then_inc(pool_dec, 1)

            def rms_step(i, j):
                s = i * 2 + j
                pool.wait_ge(dve_comb, (s + 1) * COMB_N)
                nc.gpsimd.tensor_tensor(rms[:], msn[:], neg_half[:, 0:2 * H], ALU.pow).then_inc(rms_ready, 1)

            def place_rows(i, j):
                s = i * 2 + j
                pool.wait_ge(xn_rows_ready, s + 1)
                pool.wait_ge(rows_ready, (s + 1) * 2)
                pool.sem_inc(tick, 1)
                for k in range(2):
                    nc.gpsimd.indirect_dma_start(out=sorted_dram, out_offset=bass.IndirectOffsetOnAxis(ap=pos_s[j][:, k:k + 1], axis=0),
                                                 in_=rows[j][:, k, :], in_offset=None).then_inc(placed[j], 16)

            def step(i, j):
                pool.wait_ge(dve_on, (i * 2 + j - 1) * ON_N)
                rms_step(*turn(i, j, -1, 2))
                dec(*turn(i, j, 1, 2))
                place_rows(i, j)

            pool.wait_ge(dve_route, ROUTE["gc"])
            dec(0, 0)
            dec(0, 1)
            pool.wait_ge(sort_cleared, ROWS // BR * 16)
            place_rows(0, 0)
            rms_step(0, 0)
            dec(1, 0)
            place_rows(0, 1)
            with pool.Fori(1, SEQS // 2 - 1) as i:
                for j in range(2):
                    step(i, j)
            last = SEQS // 2 - 1
            pool.wait_ge(dve_on, (LAST - 2) * ON_N)
            rms_step(last - 1, 1)
            dec(last, 1)
            place_rows(last, 0)
            place_rows(last, 1)
            pool.wait_ge(dve_on, (LAST - 1) * ON_N)
            rms_step(last, 0)
            pool.wait_ge(dve_on, LAST * ON_N)
            rms_step(last, 1)

            def scatter(i, j):
                b = i * R + j
                pool.wait_ge(dve_y, (b + 1) * Y_N)
                pool.wait_ge(sidx_ready, b + 1)
                pool.sem_inc(tick, 1)
                nc.gpsimd.indirect_dma_start(out=out_rows, out_offset=bass.IndirectOffsetOnAxis(ap=sidx[j][:], axis=0),
                                             in_=yw[j][:], in_offset=None, bounds_check=TOKENS - 1, oob_is_err=False,
                                             compute_op=ALU.add).then_inc(scattered[j], 16)

            for j in range(2):
                pool.wait_ge(res_stored[j], SEQS // 2 * 16)
            for j in range(R):
                scatter(0, j)
            with pool.Fori(1, TURNS - 1) as i:
                for j in range(R):
                    scatter(i, j)
            for j in range(TAIL):
                scatter(TURNS - 1, j)
            for j in range(R):
                pool.wait_ge(scattered[j], (TURNS if j < TAIL else TURNS - 1) * 16)

        @block.tensor
        def _(pe):
            def transposes(i, q):
                g = i * 4 + q
                pe.wait_ge(xn_ready, g + 1)
                if not (isinstance(i, int) and g < 2):
                    pe.wait_ge(xts_ready, g - 1)
                for k in range(GT):
                    last = nc.tensor.transpose(psA[:, q % 2, k * P:(k + 1) * P], xn[q][:, k, :], ident[:])
                last.then_inc(xt_ps_ready, 1)

            def logits(i, q):
                g = i * 4 + q
                pe.wait_ge(xts_ready, g + 1)
                for k in range(GT):
                    last = nc.tensor.matmul(ps_logits[:, bass.ds(g * GT + k, 1), 0:NL].rearrange("p a n -> p (a n)"), xts[q % 2][:, k * P:(k + 1) * P], wr_sb[:], start=True, stop=True)
                last.then_inc(lg_ready, 1)

            pe.wait_ge(first_consts, 3)
            transposes(0, 0)
            transposes(0, 1)
            pe.wait_ge(wr_loaded, 2 * 16)
            for q in range(2, 4):
                logits(0, q - 2)
                transposes(0, q)
            with pe.Fori(1, GROUPS // 4) as i:
                for q in range(4):
                    logits(*turn(i, q, -2, 4))
                    transposes(i, q)
            logits(GROUPS // 4 - 1, 2)
            logits(GROUPS // 4 - 1, 3)

            pe.wait_ge(small_loaded, SMALL * 16)
            nc.tensor.transpose(psO[:, 2 * P:2 * P + EXP * FC], b1_rows[:], ident[0:EXP * FC, 0:EXP * FC]).then_inc(pe_route, 1)
            pe.wait_ge(pool_consts, POOL_CONSTS)
            pe.wait_ge(dve_route, ROUTE["g"])
            for a in range(2):
                last = nc.tensor.matmul(psO[:, a * P:(a + 1) * P], g_all[:, a * P:(a + 1) * P], upto[:], start=True, stop=True)
            last.then_inc(pe_route, 1)
            nc.tensor.matmul(psQK[:, 0:TH], upto[:], g_all[:], start=True, stop=True)
            nc.tensor.matmul(psQK[:, TH:2 * TH], onesf[:], g_all[:], start=True, stop=True).then_inc(pe_route, 1)
            pe.wait_ge(dve_route, ROUTE["onehot"])
            oh = onehot[:].rearrange("p t e -> p (t e)")
            for a in range(KC):
                last = nc.tensor.matmul(psT[:, a:a + 1], oh[:, a * P:(a + 1) * P], onesb[:, 0:1], start=True, stop=True)
            last.then_inc(pe_route, 1)
            pe.wait_ge(dve_route, ROUTE["count"])
            nc.tensor.matmul(psKS[:, 0:TE], before[:], oh, start=True, stop=False)
            for a in range(KC):
                nc.tensor.matmul(psKS[:, 0:TE], count_bc[:, a, :], band[:, (KC - 1 - a) * P:(2 * KC - 1 - a) * P], start=False, stop=(a == KC - 1))
            for a in range(KC):
                last = nc.tensor.matmul(psT[:, KC:KC + EXP], count_bc[:, a, :], band[:, BAND - EXP:BAND], start=(a == 0), stop=(a == KC - 1))
            last.then_inc(pe_route, 1)
            def proj(i, j):
                s = i * 2 + j
                pe.wait_ge(hi_ready, s + 1)
                pe.wait_ge(lo_ready, s + 1)
                first = isinstance(i, int) and s == 0
                parts = [(x_hi[j], w_hi), (x_hi[j], w_lo), (x_lo[j], w_hi)]
                if not first:
                    pe.wait_ge(qk_copied, s)
                for a in range(2):
                    for n, (xp, wp) in enumerate(parts):
                        last = nc.tensor.matmul(psQK[:, a * SEQ:(a + 1) * SEQ], wp[:, a * P:(a + 1) * P], xp[:], start=(n == 0), stop=(n == 2))
                last.then_inc(qk_ready, 1)
                if not first:
                    pe.wait_ge(v_copied, s)
                    pe.wait_ge(gate_ready, s)
                for k in range(2):
                    for n, (xp, wp) in enumerate(parts):
                        last = nc.tensor.matmul(psVG[:, k, :], xp[:, k * P:(k + 1) * P], wp[:, 2 * P:], start=(n == 0), stop=(n == 2))
                last.then_inc(vg_ready, 1)

            def scores(i, j):
                s = i * 2 + j
                pe.wait_ge(qk_copied, s + 1)
                if not (isinstance(i, int) and s == 0):
                    pe.wait_ge(p_ready, s * 2)
                for k in range(2):
                    nc.tensor.matmul(psA[:, k, :], kT[:, k * P:(k + 1) * P], qb[:, k, :, :].rearrange("p h t -> p (h t)"),
                                     start=True, stop=True).then_inc(a_ready, 1)
                if not (isinstance(i, int) and s == 0):
                    pe.wait_ge(dve_comb, (s - 1) * COMB_N + 1)
                nc.tensor.transpose(psKS[:, 0:P], kT[:, 0:P], ident[:]).then_inc(k0_ready, 1)

            def outputs(i, j):
                s = i * 2 + j
                pe.wait_ge(kd_ready, s + 1)
                pe.wait_ge(v_copied, s + 1)
                nc.tensor.matmul(psKS[:, HV:2 * HV], kd[:], v_sb[j][:, 0, :], start=True, stop=True).then_inc(s_ready, 1)
                if not (isinstance(i, int) and s == 0):
                    pe.wait_ge(o_copied, s)
                for k in range(2):
                    pe.wait_ge(p_ready, s * 2 + k + 1)
                    for h in range(H):
                        last = nc.tensor.matmul(psO[:, k * HV + h * DV:k * HV + (h + 1) * DV], pr[:, k, h * P:(h + 1) * P],
                                                v_sb[j][:, k, h * DV:(h + 1) * DV], start=True, stop=True)
                last.then_inc(o_ready, 1)
                pe.wait_ge(s_copied, s + 1)
                nc.tensor.matmul(psKS[:, 0:HV], qT1[j][:], S_sb[:], start=True, stop=True).then_inc(inter_ready, 1)

            def transpose_on(i, j):
                s = i * 2 + j
                pe.wait_ge(dve_on, (s + 1) * ON_N)
                if not (isinstance(i, int) and s == 0):
                    pe.wait_ge(res_ready, s)
                for k in range(2):
                    for a in range(2):
                        last = nc.tensor.transpose(psT[:, (2 * k + a) * P:(2 * k + a + 1) * P], on[:, k, a * P:(a + 1) * P], ident[:])
                last.then_inc(oT_ps_ready, 1)

            def project_out(i, j):
                s = i * 2 + j
                pe.wait_ge(oT_copied, s + 1)
                for k in range(2):
                    for a in range(2):
                        last = nc.tensor.matmul(psT[:, k * D:(k + 1) * D], oT[:, 2 * k + a, :], wo_sb[:, a, :],
                                                start=(a == 0), stop=(a == 1))
                last.then_inc(wo_ready, 1)

            def step(i, j):
                scores(i, j)
                project_out(*turn(i, j, -2, 2))
                proj(*turn(i, j, 1, 2))
                outputs(i, j)
                transpose_on(*turn(i, j, -1, 2))

            pe.wait_ge(w_split, 6)
            pe.wait_ge(dve_route, ROUTE["gdiff"])
            proj(0, 0)
            pe.wait_ge(dve_route, ROUTE["read"])
            scores(0, 0)
            proj(0, 1)
            outputs(0, 0)
            scores(0, 1)
            proj(1, 0)
            outputs(0, 1)
            transpose_on(0, 0)
            pe.wait_ge(wo_scaled, 2)
            with pe.Fori(1, SEQS // 2 - 1) as i:
                for j in range(2):
                    step(i, j)
            psXT = [psQK, psKS]
            psY = [psO, psT]

            def transpose_rows(i, j):
                b = i * R + j
                pe.wait_ge(xg_loaded[j], (i + 1) * 16)
                if not (isinstance(i, int) and b < 2):
                    pe.wait_ge(xgT_copied, b - 1)
                nc.tensor.transpose(psXT[j % 2][:, 0:P], xg[j][:, 0:D], ident[:]).then_inc(xgT_ps_ready, 1)

            def layer1(i, j):
                b = i * R + j
                pe.wait_ge(xgT_copied, b + 1)
                pe.wait_ge(w_copied, b + 1)
                if not (isinstance(i, int) and b < 2):
                    pe.wait_ge(gelu_done, b - 1)
                for c in range(FC):
                    last = nc.tensor.matmul(psVG[:, j % 2, c * P:(c + 1) * P], wbuf[j % 4][:, c * P:(c + 1) * P], xgT[j % 2][:],
                                            start=True, stop=True)
                last.then_inc(h_ready, 1)

            def layer2(i, j, e):
                b = i * R + j
                pe.wait_ge(gelu_done, b + 1)
                if not (isinstance(i, int) and b < 2):
                    pe.wait_ge(dve_y, (b - 2) * Y_N + 1)
                for c in range(FC):
                    last = nc.tensor.matmul(psY[j % 2][:, 0:D], hid[j % 2][:, c, :],
                                            w2_sb[:, bass.ds(e, 1), c, :].rearrange("p a d -> p (a d)"),
                                            start=(c == 0), stop=(c == FC - 1))
                last.then_inc(y_ready, 1)

            def block_step(i, j):
                layer1(i, j)
                if not (isinstance(i, int) and i * R + j == 0):
                    e = pe.value_load(be[0:1, bass.ds(i * R + j - 1, 1)], min_val=0, max_val=EXP - 1)
                if not (isinstance(i, int) and i * R + j + 1 >= BLOCKS):
                    transpose_rows(*turn(i, j, 1, R))
                if not (isinstance(i, int) and i * R + j == 0):
                    layer2(*turn(i, j, -1, R), e)

            last = SEQS // 2 - 1
            step(last, 0)
            scores(last, 1)
            project_out(last - 1, 1)
            outputs(last, 1)
            transpose_on(last, 0)
            project_out(last, 0)
            pe.wait_ge(dve_late, 8)
            pe.wait_ge(w_loaded, W_LOADS * 16)
            pe.wait_ge(gate_ready, SEQS)
            transpose_rows(0, 0)
            pe.wait_ge(dve_comb, LAST * COMB_N + 1)
            block_step(0, 0)
            transpose_on(last, 1)
            block_step(0, 1)
            project_out(last, 1)
            pe.wait_ge(res_ready, SEQS)
            for j in range(2, R):
                block_step(0, j)
            with pe.Fori(1, TURNS - 1) as i:
                for j in range(R):
                    block_step(i, j)
            for j in range(TAIL):
                block_step(TURNS - 1, j)
            layer2(TURNS - 1, TAIL - 1, pe.value_load(be[0:1, BLOCKS - 1:BLOCKS], min_val=0, max_val=EXP - 1))

        @block.scalar
        def _(act):
            act.dma_start(wr_sb[:, 0:EXP], gate_w).then_inc(wr_loaded, 16)
            act.dma_start(wr_sb[:, EXP:NL], Wgk).then_inc(wr_loaded, 16)

            act.wait_ge(first_consts, 2)
            nc.scalar.activation(warm[:], neg_half[:], ACT.Exp)

            def copy_xt(i, q):
                g = i * 4 + q
                act.wait_ge(xt_ps_ready, g + 1)
                if not (isinstance(i, int) and g < 2):
                    s2, t2 = (q % 2, i * 2 + q // 2)
                    act.wait_ge(xt_stored[s2], t2 * 16)
                    act.wait_ge(lg_ready, g - 1)
                nc.scalar.copy(xts[q % 2][:], psA[:, q % 2, :]).then_inc(xts_ready, 1)

            def norm_tile(to, t):
                return nc.scalar.activation(to, x_all[:, bass.ds(t, 1), :].rearrange("p a d -> p (a d)"), ACT.Identity,
                                            bias=nmr[:, bass.ds(t, 1)], scale=rstd[:, bass.ds(t, 1)])

            def apply_norm(i, q):
                g = i * 4 + q
                act.wait_ge(nmr_ready, g + 1)
                if not (isinstance(i, int) and i == 0):
                    act.wait_ge(xt_ps_ready, g - 3)
                for k in range(GT):
                    last = norm_tile(xn[q][:, k, :], g * GT + k)
                last.then_inc(xn_ready, 1)

            def norm_step(i, q):
                apply_norm(i, q)
                if not (isinstance(i, int) and i * 4 + q < 1):
                    copy_xt(*turn(i, q, -1, 4))

            for q in range(4):
                norm_step(0, q)
            with act.Fori(1, GROUPS // 4) as i:
                for q in range(4):
                    norm_step(i, q)
            last = GROUPS // 4 - 1
            copy_xt(last, 3)

            for j in range(2):
                act.wait_ge(xT_loaded[j], 16)
                nc.scalar.copy(x_hi[j][:], xT[j][:]).then_inc(hi_ready, 1)

            act.wait_ge(dve_route, ROUTE["az"])
            nc.scalar.activation(ez[:], az[:], ACT.Exp, scale=-1.0).then_inc(act_route, 1)
            act.wait_ge(act_route, 1)
            nc.scalar.activation(l1[:], ez[:], ACT.Ln, bias=onesf[:, 0:1]).then_inc(act_route, 1)
            act.wait_ge(pe_route, 2)
            nc.scalar.copy(gcT[:].rearrange("p a t -> p (a t)"), psO[:, 0:2 * P]).then_inc(act_route, 1)
            nc.scalar.copy(w1b[:, :, FF:FF + FC], psO[:, 2 * P:2 * P + EXP * FC].rearrange("p (e c) -> p e c", c=FC)).then_inc(act_route, 1)
            act.wait_ge(dve_route, ROUTE["gdiff"])
            nc.scalar.activation(e_k[:].rearrange("p t h -> p (t h)"), gdiff[:], ACT.Exp).then_inc(act_route, 1)
            nc.scalar.activation(e_q[:].rearrange("p t h -> p (t h)"), gc[:].rearrange("p t h -> p (t h)"), ACT.Exp).then_inc(act_route, 1)

            act.wait_ge(dve_route, ROUTE["d"])
            nc.scalar.activation(ex[:], d_all[:], ACT.Exp).then_inc(act_route, 1)

            def copy_qk(i, j):
                s = i * 2 + j
                act.wait_ge(qk_ready, s + 1)
                if not (isinstance(i, int) and s == 0):
                    act.wait_ge(k0_ready, s)
                for h in range(H):
                    r = slice(h * DK, (h + 1) * DK)
                    nc.scalar.activation(qb[r, :, h, :], psQK[r, 0:SEQ].rearrange("p (k t) -> p k t", k=2), ACT.Copy, scale=float(DK) ** -0.5)
                if not (isinstance(i, int) and s < 2):
                    act.wait_ge(inter_ready, s - 1)
                nc.scalar.activation(qT1[j][:], psQK[:, P:SEQ], ACT.Copy, scale=float(DK) ** -0.5)
                nc.scalar.copy(kT[:], psQK[:, SEQ:2 * SEQ]).then_inc(qk_copied, 1)

            def tanh(i, j):
                s = i * 2 + j
                act.wait_ge(vg_ready, s + 1)
                if not (isinstance(i, int) and s == 0):
                    act.wait_ge(gate_ready, s)
                nc.scalar.activation(th[:], psVG[:, :, HV:2 * HV], ACT.Tanh, scale=0.5)

            def copy_v(i, j):
                s = i * 2 + j
                if not (isinstance(i, int) and s < 2):
                    act.wait_ge(o_ready, s - 1)
                nc.scalar.copy(v_sb[j][:], psVG[:, :, 0:HV]).then_inc(v_copied, 1)

            def exp_dec(i, j):
                s = i * 2 + j
                act.wait_ge(pool_dec, (s + 1) * 2)
                if not (isinstance(i, int) and s < 2):
                    act.wait_ge(p_ready, (s - 1) * 2)
                nc.scalar.activation(E[j][:].rearrange("p k n -> p (k n)"), gcB[j][:].rearrange("p h t -> p (h t)"), ACT.Exp).then_inc(e_ready, 1)

            def copy_o(i, j):
                s = i * 2 + j
                act.wait_ge(o_ready, s + 1)
                if not (isinstance(i, int) and s == 0):
                    act.wait_ge(dve_on, (s - 1) * ON_N + 1)
                nc.scalar.copy(oo[:].rearrange("p k n -> p (k n)"), psO[:]).then_inc(o_copied, 1)

            def copy_oT(i, j):
                s = i * 2 + j
                act.wait_ge(oT_ps_ready, s + 1)
                if not (isinstance(i, int) and s == 0):
                    act.wait_ge(wo_ready, s)
                nc.scalar.copy(oT[:].rearrange("p a t -> p (a t)"), psT[:]).then_inc(oT_copied, 1)

            def split_hi(i, j):
                act.wait_ge(xT_loaded[j], (i + 1) * 16)
                nc.scalar.copy(x_hi[j][:], xT[j][:]).then_inc(hi_ready, 1)

            def norm_rows(i, j):
                s = i * 2 + j
                if not (isinstance(i, int) and s < 2):
                    act.wait_ge(placed[j], i * 32)
                for k in range(2):
                    last = norm_tile(rows[j][:, k, 0:D], s * 2 + k)
                last.then_inc(xn_rows_ready, 1)

            norm_rows(0, 0)
            copy_qk(0, 0)
            tanh(0, 0)
            copy_v(0, 0)
            exp_dec(0, 0)
            copy_qk(0, 1)
            tanh(0, 1)
            copy_v(0, 1)

            def step(i, j):
                exp_dec(*turn(i, j, 1, 2))
                copy_qk(*turn(i, j, 2, 2))
                tanh(*turn(i, j, 2, 2))
                copy_v(*turn(i, j, 2, 2))
                norm_rows(*turn(i, j, 2, 2))
                if not (isinstance(i, int) and i * 2 + j + 3 > LAST):
                    split_hi(*turn(i, j, 3, 2))
                copy_o(*turn(i, j, 1, 2))
                copy_oT(i, j)

            split_hi(1, 0)
            norm_rows(0, 1)
            copy_o(0, 0)
            step(0, 0)
            step(0, 1)
            with act.Fori(1, SEQS // 2 - 2) as i:
                for j in range(2):
                    step(i, j)
            psXT = [psQK, psKS]

            def copy_rows(i, j):
                b = i * R + j
                act.wait_ge(xgT_ps_ready, b + 1)
                if not (isinstance(i, int) and b < 2):
                    act.wait_ge(h_ready, b - 1)
                nc.scalar.copy(xgT[j % 2][:], psXT[j % 2][:, 0:P]).then_inc(xgT_copied, 1)

            def gelu(i, j):
                b = i * R + j
                act.wait_ge(h_ready, b + 1)
                if not (isinstance(i, int) and b < 2):
                    act.wait_ge(y_ready, b - 1)
                if isinstance(i, int) and b < 2:
                    act.wait_ge(*[(dve_comb, SEQS * COMB_N), (dve_on, SEQS * ON_N)][b])
                for c in range(FC):
                    last = nc.scalar.activation(hid[j % 2][:, c, :], psVG[:, j % 2, c * P:(c + 1) * P], ACT.Gelu,
                                                bias=wbuf[j % 4][:, FF + c:FF + c + 1])
                last.then_inc(gelu_done, 1)

            def block_step(i, j):
                if not (isinstance(i, int) and i * R + j + 1 >= BLOCKS):
                    copy_rows(*turn(i, j, 1, R))
                gelu(i, j)

            last = SEQS // 2 - 1
            step(last - 1, 0)
            step(last - 1, 1)
            exp_dec(last, 1)
            copy_o(last, 1)
            copy_oT(last, 0)
            copy_rows(0, 0)
            block_step(0, 0)
            copy_oT(last, 1)
            for j in range(1, R):
                block_step(0, j)
            with act.Fori(1, TURNS - 1) as i:
                for j in range(R):
                    block_step(i, j)
            for j in range(TAIL):
                block_step(TURNS - 1, j)

        @block.vector
        def _(dve):
            c_stats = Chain(dve, dve_stats, STATS_N)

            def statistics(i, q):
                g = i * 4 + q
                c_stats.begin(g)
                dve.wait_ge(x_loaded[q], (i + 1) * 16)
                for k in range(GT):
                    c_stats.up(nc.vector.bn_stats(stats[q][:, k, :], x_all[:, bass.ds(g * GT + k, 1), :].rearrange("p a d -> p (a d)")))
                c_stats.wait()
                dve.sem_inc(tick, 1)
                for k in range(GT):
                    c_stats.up(nc.vector.bn_aggr(mv[q][:, k, :], stats[q][:, k, :]))
                c_stats.wait()
                c_stats.up(nc.vector.tensor_scalar(vpe[q][:], mv[q][:, :, 1], LN_EPS, None, ALU.add))
                c_stats.end()

            def mean_term(i, q):
                g = i * 4 + q
                dve.wait_ge(rstd_ready, g + 1)
                at = bass.ds(g * GT, GT)
                nc.vector.scalar_tensor_tensor(nmr[:, at], mv[q][:, :, 0], -1.0, rstd[:, at], ALU.mult, ALU.mult).then_inc(nmr_ready, 1)

            def norm_step(i, q):
                if not (isinstance(i, int) and i * 4 + q + 1 >= GROUPS):
                    statistics(*turn(i, q, 1, 4))
                mean_term(i, q)

            statistics(0, 0)
            for q in range(4):
                norm_step(0, q)
                if q == 0:
                    dve.wait_ge(pool_consts, 1)
                    nc.vector.tensor_scalar(band_i[:], band_i[:], EXP - 1, None, ALU.bitwise_and).then_inc(band_step, 1)
                    dve.wait_ge(band_step, 1)
                    nc.vector.tensor_scalar(band[:], band_i[:], 0, None, ALU.is_equal).then_inc(first_band, 1)
            with dve.Fori(1, GROUPS // 4 - 1) as i:
                for q in range(4):
                    norm_step(i, q)
            last = GROUPS // 4 - 1
            for q in range(4):
                norm_step(last, q)
            def split_lo(i, j):
                s = i * 2 + j
                dve.wait_ge(hi_ready, s + 1)
                nc.vector.tensor_tensor(x_lo[j][:], xT[j][:], x_hi[j][:].bitcast(F32), ALU.subtract).then_inc(lo_ready, 1)

            c = Chain(dve, dve_route, 0)
            c.begin(0)

            def then(ins, name=None):
                c.up(ins)
                if name:
                    assert ROUTE[name] == c.n, (name, c.n)
                c.wait()

            def bc(ap, shape):
                return ap.to_broadcast(shape)

            zf = z[:].rearrange("p t h -> p (t h)")

            def decay_logits(t):
                n = TILES // 2
                zt, f = z[:, t:t + n, :], slice(t * H, (t + n) * H)
                then(nc.vector.tensor_tensor(zt, ps_logits[:, t:t + n, EXP:NL], bc(bgk_bc[:].unsqueeze(1), [P, n, H]), ALU.add))
                then(nc.vector.scalar_tensor_tensor(az[:, f], zf[:, f], -1.0, zf[:, f], ALU.mult, ALU.max), "az" if t else None)

            def router_logits(t):
                n = TILES // 2
                m, d, lg = lmax[:, t:t + n], d_all[:, t:t + n, :], ps_logits[:, t:t + n, 0:EXP]
                then(nc.vector.tensor_reduce(m, lg, AX.X, ALU.max))
                then(nc.vector.tensor_tensor(d, lg, bc(m.unsqueeze(2), [P, n, EXP]), ALU.subtract), "d" if t else None)

            def choose(t):
                n = TILES // 2
                v, m = val[:, t:t + n, :], vmax[:, t:t + n]
                then(nc.vector.scalar_tensor_tensor(v, d_all[:, t:t + n, :], 0.0, bc(rev[:].unsqueeze(1), [P, n, EXP]), ALU.is_equal, ALU.mult))
                then(nc.vector.tensor_reduce(m, v, AX.X, ALU.max))
                then(nc.vector.tensor_tensor(onehot[:, t:t + n, :], v, bc(m.unsqueeze(2), [P, n, EXP]), ALU.is_equal), "onehot" if t else None)

            dve.wait_ge(lg_ready, GROUPS // 2)
            dve.wait_ge(small_loaded, SMALL * 16)
            dve.wait_ge(pool_consts, POOL_CONSTS)
            then(nc.vector.tensor_copy(rev[:], rev_i[:]))
            decay_logits(0)
            router_logits(0)
            choose(0)
            dve.wait_ge(proj_loaded, 16 * 5)
            weights = [(wq_sb, 0, P), (wk_sb, P, 2 * P), (wvg_sb, 2 * P, 2 * P + 2 * HV)]
            for w, a, b in weights:
                nc.vector.tensor_copy(w_hi[:, a:b], w[:]).then_inc(w_split, 1)
            dve.wait_ge(w_split, 3)
            for w, a, b in weights:
                nc.vector.tensor_tensor(w_lo[:, a:b], w[:], w_hi[:, a:b].bitcast(F32), ALU.subtract).then_inc(w_split, 1)

            split_lo(0, 0)
            split_lo(0, 1)
            dve.wait_ge(lg_ready, GROUPS)
            decay_logits(TILES // 2)
            router_logits(TILES // 2)
            dve.wait_ge(act_route, 2)
            then(nc.vector.scalar_tensor_tensor(g_all[:], zf, 0.0, l1[:], ALU.min, ALU.subtract))
            then(nc.vector.tensor_scalar(g_all[:], g_all[:], 1.0 / GATE_NORM, None, ALU.mult), "g")
            choose(TILES // 2)
            gcf = gc[:].rearrange("p t h -> p (t h)")
            dve.wait_ge(pe_route, 3)
            then(nc.vector.tensor_copy(gcf, psQK[:, 0:TH]), "gc")
            then(nc.vector.tensor_tensor(gdiff[:], psQK[:, TH:2 * TH], gcf, ALU.subtract), "gdiff")
            dve.wait_ge(pe_route, 4)
            then(nc.vector.tensor_copy(count[:], psT[:, 0:KC]))
            then(nc.vector.tensor_copy(count_bc[:], bc(count[:].unsqueeze(2), [P, KC, P])), "count")
            dve.wait_ge(pe_route, 5)
            then(nc.vector.tensor_scalar(tot_i[:], psT[:, KC:KC + EXP], float(P - 1), None, ALU.add))
            then(nc.vector.tensor_scalar(nb_i[:], tot_i[:], P.bit_length() - 1, None, ALU.arith_shift_right))
            then(nc.vector.tensor_copy(cb[0][:, EXP:], nb_i[:]))
            k, a = 1, 0
            while k < EXP:
                then(nc.vector.tensor_tensor(cb[1 - a][:, EXP:], cb[a][:, EXP:], cb[a][:, EXP - k:2 * EXP - k], ALU.add))
                k, a = 2 * k, 1 - a
            upto_e = cb[a][:, EXP:]
            then(nc.vector.tensor_scalar(base[:], cb[a][:, EXP - 1:2 * EXP - 1], float(P), None, ALU.mult))
            then(nc.vector.tensor_tensor(slot_f[:], psKS[:, 0:TE].rearrange("p (t e) -> p t e", e=EXP),
                                         bc(base[:].unsqueeze(1), [P, TILES, EXP]), ALU.add), "read")
            then(nc.vector.tensor_tensor(slot_f[:], slot_f[:], onehot[:], ALU.mult))
            then(nc.vector.tensor_reduce(pos[:], slot_f[:], AX.X, ALU.add), "all")
            dve.wait_ge(act_route, 6)

            c_late = Chain(dve, dve_late, 8)
            c_late.begin(0)

            def late(ins):
                c_late.up(ins)
                c_late.wait()

            def sort_data():
                late(nc.vector.tensor_copy(pos_i[:], pos[:]))
                late(nc.vector.tensor_copy(extra[:, :, 1], ids[:]))
                dve.wait_ge(act_route, 7)
                late(nc.vector.tensor_reduce(sumex[:], ex[:], AX.X, ALU.add))
                late(nc.vector.reciprocal(extra[:, :, 0], sumex[:]))

            def scale_wo():
                dve.wait_ge(proj_loaded, 16 * 5)
                for a in range(2):
                    nc.vector.tensor_scalar(wo_sb[:, a, :], wo_raw[:, a, :], gn_col[:, 0:1], 0.5, ALU.mult, ALU.mult).then_inc(wo_scaled, 1)

            def block_experts():
                late(nc.vector.tensor_copy(iota_f[:], iota_i[:]))
                late(nc.vector.tensor_tensor(isge[:], bc(iota_f[:, 0:BLOCKS].unsqueeze(2), [P, BLOCKS, EXP - 1]),
                                             bc(upto_e[:, 0:EXP - 1].unsqueeze(1), [P, BLOCKS, EXP - 1]), ALU.is_ge))
                late(nc.vector.tensor_reduce(be_f[:], isge[:], AX.X, ALU.add))
                late(nc.vector.tensor_copy(be[:], be_f[:]))

            def add_extra(i, j):
                s = i * 2 + j
                if not (isinstance(i, int) and s < 2):
                    dve.wait_ge(placed[j], i * 32)
                nc.vector.tensor_copy(pos_s[j][:], pos_i[:, bass.ds(s * 2, 2)]).then_inc(rows_ready, 1)
                nc.vector.tensor_copy(rows[j][:, :, D:XW], extra[:, bass.ds(s * 2, 2), :]).then_inc(rows_ready, 1)

            c_comb = Chain(dve, dve_comb, COMB_N)
            c_on = Chain(dve, dve_on, ON_N)

            def combine(i, j):
                s = i * 2 + j
                c_comb.begin(s)
                dve.wait_ge(inter_ready, s + 1)
                c_comb.up(nc.vector.tensor_tensor(inter[:].rearrange("p (h d) -> p h d", d=DV), psKS[:, 0:HV].rearrange("p (h d) -> p h d", d=DV),
                                                  bc(e_q[:, bass.ds(s * 2 + 1, 1), :].rearrange("p a h -> p (a h)").unsqueeze(2), [P, H, DV]), ALU.mult))
                c_comb.wait()
                dve.wait_ge(o_copied, s + 1)
                c_comb.up(nc.vector.tensor_tensor(oo[:, 1, :], inter[:], oo[:, 1, :], ALU.add))
                c_comb.wait()
                c_comb.up(nc.vector.tensor_tensor(sq[:], oo[:], oo[:], ALU.mult))
                c_comb.wait()
                c_comb.up(nc.vector.tensor_reduce(ms[:], sq[:].rearrange("p k (h d) -> p (k h) d", d=DV), AX.X, ALU.add))
                c_comb.wait()
                c_comb.up(nc.vector.tensor_scalar(msn[:], ms[:], 1.0 / DV, RMS_EPS, ALU.mult, ALU.add))
                c_comb.end()

            def probs(i, j):
                s = i * 2 + j
                dve.wait_ge(e_ready, s + 1)
                if not (isinstance(i, int) and s == 0):
                    dve.wait_ge(o_ready, s)
                for k in range(2):
                    dve.wait_ge(a_ready, s * 2 + k + 1)
                    nc.vector.tensor_tensor(pr[:, k, :], psA[:, k, :], E[j][:, k, :], ALU.mult).then_inc(p_ready, 1)

            def decay_k(i, j):
                s = i * 2 + j
                dve.wait_ge(k0_ready, s + 1)
                nc.vector.tensor_tensor(kd[:].rearrange("p (h d) -> p h d", d=DK), psKS[:, 0:P].rearrange("p (h d) -> p h d", d=DK),
                                        bc(e_k[:, bass.ds(s * 2, 1), :].rearrange("p a h -> p (a h)").unsqueeze(2), [P, H, DK]), ALU.mult).then_inc(kd_ready, 1)

            def normed(i, j):
                s = i * 2 + j
                c_on.begin(s)
                c_on.up(nc.vector.tensor_tensor(og[:], oo[:], gate[j][:], ALU.mult))
                c_on.wait()
                dve.wait_ge(rms_ready, s + 1)
                if not (isinstance(i, int) and s == 0):
                    dve.wait_ge(oT_ps_ready, s)
                c_on.up(nc.vector.tensor_tensor(on[:].rearrange("p k (h d) -> p (k h) d", d=DV), og[:].rearrange("p k (h d) -> p (k h) d", d=DV),
                                                bc(rms[:].unsqueeze(2), [P, 2 * H, DV]), ALU.mult))
                c_on.end()

            def copy_state(i, j):
                s = i * 2 + j
                dve.wait_ge(s_ready, s + 1)
                if not (isinstance(i, int) and s == 0):
                    dve.wait_ge(inter_ready, s)
                nc.vector.tensor_tensor(S_sb[:], psKS[:, HV:2 * HV], headmask[:], ALU.mult).then_inc(s_copied, 1)

            def make_gate(i, j):
                s = i * 2 + j
                dve.wait_ge(v_copied, s + 1)
                nc.vector.scalar_tensor_tensor(gate[j][:], th[:], 1.0, psVG[:, :, HV:2 * HV], ALU.add, ALU.mult).then_inc(gate_ready, 1)

            def residual(i, j):
                s = i * 2 + j
                dve.wait_ge(wo_ready, s + 1)
                if not (isinstance(i, int) and s < 2):
                    dve.wait_ge(res_stored[j], i * 16)
                nc.vector.tensor_tensor(res[j][:], psT[:, 0:2 * D].rearrange("p (k d) -> p k d", d=D), x_all[:, bass.ds(s * 2, 2), :],
                                        ALU.add).then_inc(res_ready, 1)

            make_gate(0, 0)
            probs(0, 0)
            decay_k(0, 0)
            sort_data()
            copy_state(0, 0)
            make_gate(0, 1)
            split_lo(1, 0)
            add_extra(0, 0)
            add_extra(0, 1)
            scale_wo()
            combine(0, 0)
            probs(0, 1)
            decay_k(0, 1)
            normed(0, 0)
            copy_state(0, 1)
            split_lo(1, 1)
            make_gate(1, 0)
            block_experts()
            c_late.end()

            def step(i, j):
                combine(*turn(i, j, -1, 2))
                decay_k(i, j)
                probs(i, j)
                normed(*turn(i, j, -1, 2))
                copy_state(i, j)
                residual(i - 1, j)
                make_gate(*turn(i, j, 1, 2))
                split_lo(*turn(i, j, 2, 2))
                add_extra(i, j)

            with dve.Fori(1, SEQS // 2 - 1) as i:
                for j in range(2):
                    step(i, j)
            c_y = Chain(dve, dve_y, Y_N)
            psY = [psO, psT]

            def expert_of(i, j):
                return dve.value_load(be[0:1, bass.ds(i * R + j, 1)], min_val=0, max_val=EXP - 1)

            def copy_w(i, j, e):
                b = i * R + j
                if not (isinstance(i, int) and b < 4):
                    dve.wait_ge(gelu_done, b - 3)
                nc.vector.tensor_copy(wbuf[j % 4], w1b[:, bass.ds(e, 1), :].rearrange("p a n -> p (a n)")).then_inc(w_copied, 1)

            def weigh(i, j):
                b = i * R + j
                c_y.begin(b)
                if not (isinstance(i, int) and i == 0):
                    dve.wait_ge(scattered[j], i * 16)
                dve.wait_ge(xg_loaded[j], (i + 1) * 16)
                nc.vector.tensor_copy(sidx[j][:], xg[j][:, D + 1:XW]).then_inc(sidx_ready, 1)
                dve.wait_ge(y_ready, b + 1)
                c_y.up(nc.vector.tensor_tensor(yb[j % 2][:], psY[j % 2][:, 0:D], wbuf[j % 4][:, FF + FC:WB], ALU.add))
                c_y.wait()
                c_y.up(nc.vector.tensor_scalar(yw[j][:], yb[j % 2][:], xg[j][:, D:D + 1], None, ALU.mult))
                c_y.end()

            last = SEQS // 2 - 1
            combine(last - 1, 1)
            probs(last, 0)
            decay_k(last, 0)
            normed(last - 1, 1)
            copy_state(last, 0)
            make_gate(last, 1)
            residual(last - 1, 0)
            add_extra(last, 0)
            add_extra(last, 1)
            combine(last, 0)
            probs(last, 1)
            decay_k(last, 1)
            residual(last - 1, 1)
            normed(last, 0)
            copy_state(last, 1)
            dve.wait_ge(w_loaded, W_LOADS * 16)
            dve.wait_ge(p_ready, SEQS * 2)
            copy_w(0, 0, expert_of(0, 0))
            combine(last, 1)
            copy_w(0, 1, expert_of(0, 1))
            normed(last, 1)
            residual(last, 0)
            copy_w(0, 2, expert_of(0, 2))
            e = expert_of(0, 3)
            residual(last, 1)

            def block_step(i, j, e):
                if not (isinstance(i, int) and i * R + j + 3 >= BLOCKS):
                    copy_w(*turn(i, j, 3, R), e)
                if j + 1 < R and not (isinstance(i, int) and i * R + j + 4 >= BLOCKS):
                    e = expert_of(*turn(i, j, 4, R))
                weigh(i, j)
                return e

            for j in range(R):
                e = block_step(0, j, e)
            with dve.Fori(1, TURNS - 1) as i:
                e = expert_of(*turn(i, 0, 3, R))
                for j in range(R):
                    e = block_step(i, j, e)
            e = expert_of(TURNS - 1, 3)
            for j in range(TAIL):
                e = block_step(TURNS - 1, j, e)


POOL_CONSTS = 19
SMALL = 4
ROUTE = {"az": 10, "d": 12, "g": 14, "onehot": 17, "gc": 18, "gdiff": 19, "count": 21, "read": 29, "all": 31}


_INS = ["L0_attn_x", "L0_attn_Wq", "L0_attn_Wk", "L0_attn_Wv", "L0_attn_Wg", "L0_attn_Wgk", "L0_attn_bgk", "L0_attn_Wo",
        "L0_attn_gnorm_w", "L0_ffn_gate_w", "L0_ffn_w1", "L0_ffn_b1", "L0_ffn_w2", "L0_ffn_b2"]


def kernel(**inputs):
    import numpy as _np
    import concourse.bacc as _bacc
    from concourse import mybir as _mybir
    from concourse.bass_utils import run_bass_kernel_spmd as _run

    nc = _bacc.Bacc("TRN2", target_bir_lowering=False, num_devices=1)
    arrays, args = {}, []
    for name in _INS:
        a = _np.ascontiguousarray(inputs[name])
        arrays[f"in_{name}_dram"] = a
        args.append(nc.dram_tensor(f"in_{name}_dram", a.shape, _mybir.dt.from_np(a.dtype), kind="ExternalInput").ap())
    shape = inputs["L0_attn_x"].shape
    args.append(nc.dram_tensor("out_0_dram", shape, _mybir.dt.float32, kind="ExternalOutput").ap())
    build_layer(nc, *args)
    r = _run(nc, [arrays], core_ids=[0])
    return r.results[0]["out_0_dram"]
```
